# Optimizing a Trainium2 kernel written in Bass

```python
import numpy as np
import jax
import jax.numpy as jnp

def _softmax(x, axis=-1):
    return jax.nn.softmax(x, axis=axis)

def _gelu(x):
    return jax.nn.gelu(x, approximate=True)

def _silu(x):
    return jax.nn.silu(x)

def _sigmoid(x):
    return jax.nn.sigmoid(x)

def _layernorm(x, axis=-1, eps=1e-05):
    m = jnp.mean(x, axis=axis, keepdims=True)
    v = jnp.var(x, axis=axis, keepdims=True)
    return (x - m) / jnp.sqrt(v + eps)

def _scatter_add(tgt, idx, src, axis=0):
    return tgt.at[idx].add(src)

def _segment_sum(src, seg, n):
    return jax.ops.segment_sum(src, seg, n)
kernel_name = 'mk_cond_seq_d1_seqx_r2_165ddc'

def setup_inputs(seed: int=0):
    np.random.seed(seed)
    _w = jnp.asarray

    def _rec_inputs():
        import jax
        import jax.numpy as jnp
        _rk = jax.random.key(seed)
        x = -0.0003929 + 0.9999 * jax.random.normal(jax.random.fold_in(_rk, 1), (32, 512, 512), jnp.float32)
        _lenS = 512 - jax.random.randint(jax.random.fold_in(_rk, 7), (32,), 0, max(1, 512 // 4) + 1, jnp.int32)
        _lenS2 = 512 - jax.random.randint(jax.random.fold_in(_rk, 8), (32,), 0, max(1, 512 // 4) + 1, jnp.int32)
        cond_1024 = 0.00782532 + 1.00527 * jax.random.normal(jax.random.fold_in(_rk, 11), (32, 512), jnp.float32)
        _validS = jnp.arange(512)[None, :] < _lenS[:, None]
        _validS2 = jnp.arange(512)[None, :] < _lenS2[:, None]
        _causal = jnp.tril(jnp.ones((512, 512), dtype=bool))
        mask_BxS_bk0 = jnp.logical_not(jnp.broadcast_to(_validS[:, :], (32, 512)))
        return (x, cond_1024, mask_BxS_bk0)
    x, cond_1024, mask_BxS_bk0 = _rec_inputs()

    def _L0_cond_setup():
        import jax, jax.numpy as jnp
        import numpy as np
        B, L, D = (8, 1024, 512)
        FF_MULT = 2
        EPS = 1e-06

        def _layernorm(x):
            mu = jnp.mean(x, axis=-1, keepdims=True)
            var = jnp.mean(jnp.square(x - mu), axis=-1, keepdims=True)
            return (x - mu) / jnp.sqrt(var + EPS)

        def _ssm_fallback(u, w1, b1, w2, b2):
            h = jax.nn.gelu(u @ w1 + b1, approximate=False)
            return h @ w2 + b2
        key = jax.random.key(seed)
        ks = jax.random.split(key, 20)
        s = 0.02
        inp = {'x': jax.random.normal(ks[0], (B, L, D), jnp.float32), 't': jax.random.normal(ks[1], (B, D), jnp.float32), 'mask': jax.random.randint(ks[2], (B, L), 0, 2) > 0, 'ada_w': jax.random.normal(ks[3], (D, 3 * D), jnp.float32) * s, 'ada_b': jnp.zeros((3 * D,), jnp.float32), 'ssm_w1': jax.random.normal(ks[4], (D, D), jnp.float32) * s, 'ssm_b1': jnp.zeros((D,), jnp.float32), 'ssm_w2': jax.random.normal(ks[5], (D, D), jnp.float32) * s, 'ssm_b2': jnp.zeros((D,), jnp.float32), 'bwd_w1': jax.random.normal(ks[6], (D, D), jnp.float32) * s, 'bwd_b1': jnp.zeros((D,), jnp.float32), 'bwd_w2': jax.random.normal(ks[7], (D, D), jnp.float32) * s, 'bwd_b2': jnp.zeros((D,), jnp.float32), 'ffada_w': jax.random.normal(ks[8], (D, 3 * D), jnp.float32) * s, 'ffada_b': jnp.zeros((3 * D,), jnp.float32), 'ff_w1': jax.random.normal(ks[9], (D, FF_MULT * D), jnp.float32) * s, 'ff_b1': jnp.zeros((FF_MULT * D,), jnp.float32), 'ff_w2': jax.random.normal(ks[10], (FF_MULT * D, D), jnp.float32) * s, 'ff_b2': jnp.zeros((D,), jnp.float32)}
        return inp
    _L0_cond_all = _L0_cond_setup()
    _L0_cond_in = {k: v for k, v in _L0_cond_all.items() if k in ('ada_w', 'ada_b', 'ssm_w1', 'ssm_b1', 'ssm_w2', 'ssm_b2', 'bwd_w1', 'bwd_b1', 'bwd_w2', 'bwd_b2', 'ffada_w', 'ffada_b', 'ff_w1', 'ff_b1', 'ff_w2', 'ff_b2')}
    del _L0_cond_all
    return {'x': x, 'cond_1024': cond_1024, 'mask_BxS_bk0': mask_BxS_bk0, 'L0_cond_ada_w': _L0_cond_in['ada_w'], 'L0_cond_ada_b': _L0_cond_in['ada_b'], 'L0_cond_ssm_w1': _L0_cond_in['ssm_w1'], 'L0_cond_ssm_b1': _L0_cond_in['ssm_b1'], 'L0_cond_ssm_w2': _L0_cond_in['ssm_w2'], 'L0_cond_ssm_b2': _L0_cond_in['ssm_b2'], 'L0_cond_bwd_w1': _L0_cond_in['bwd_w1'], 'L0_cond_bwd_b1': _L0_cond_in['bwd_b1'], 'L0_cond_bwd_w2': _L0_cond_in['bwd_w2'], 'L0_cond_bwd_b2': _L0_cond_in['bwd_b2'], 'L0_cond_ffada_w': _L0_cond_in['ffada_w'], 'L0_cond_ffada_b': _L0_cond_in['ffada_b'], 'L0_cond_ff_w1': _L0_cond_in['ff_w1'], 'L0_cond_ff_b1': _L0_cond_in['ff_b1'], 'L0_cond_ff_w2': _L0_cond_in['ff_w2'], 'L0_cond_ff_b2': _L0_cond_in['ff_b2']}

def reference(x, cond_1024, mask_BxS_bk0, L0_cond_ada_w, L0_cond_ada_b, L0_cond_ssm_w1, L0_cond_ssm_b1, L0_cond_ssm_w2, L0_cond_ssm_b2, L0_cond_bwd_w1, L0_cond_bwd_b1, L0_cond_bwd_w2, L0_cond_bwd_b2, L0_cond_ffada_w, L0_cond_ffada_b, L0_cond_ff_w1, L0_cond_ff_b1, L0_cond_ff_w2, L0_cond_ff_b2):
    import jax
    import jax.numpy as jnp

    def _L0_cond_ref(x, t, mask, ada_w, ada_b, ssm_w1, ssm_b1, ssm_w2, ssm_b2, bwd_w1, bwd_b1, bwd_w2, bwd_b2, ffada_w, ffada_b, ff_w1, ff_b1, ff_w2, ff_b2):
        import jax, jax.numpy as jnp
        import numpy as np
        B, L, D = (8, 1024, 512)
        FF_MULT = 2
        EPS = 1e-06

        def _layernorm(x):
            mu = jnp.mean(x, axis=-1, keepdims=True)
            var = jnp.mean(jnp.square(x - mu), axis=-1, keepdims=True)
            return (x - mu) / jnp.sqrt(var + EPS)

        def _ssm_fallback(u, w1, b1, w2, b2):
            h = jax.nn.gelu(u @ w1 + b1, approximate=False)
            return h @ w2 + b2
        m = mask[:, :, None]
        emb = jax.nn.silu(t) @ ada_w + ada_b
        shift, scale, gate_msa = jnp.split(emb, 3, axis=1)
        norm = _layernorm(x) * (1.0 + scale[:, None]) + shift[:, None]
        norm = jnp.where(m, norm, 0.0)
        fwd = _ssm_fallback(norm, ssm_w1, ssm_b1, ssm_w2, ssm_b2)
        bwd = jnp.flip(_ssm_fallback(jnp.flip(norm, axis=1), bwd_w1, bwd_b1, bwd_w2, bwd_b2), axis=1)
        ssm_out = jnp.where(m, fwd + bwd, 0.0)
        x = x + gate_msa[:, None] * ssm_out
        ff_ada = jax.nn.silu(t) @ ffada_w + ffada_b
        shift_mlp, scale_mlp, gate_mlp = jnp.split(ff_ada, 3, axis=1)
        ff_norm = _layernorm(x) * (1.0 + scale_mlp[:, None]) + shift_mlp[:, None]
        h = jax.nn.gelu(ff_norm @ ff_w1 + ff_b1, approximate=True)
        ff_out = h @ ff_w2 + ff_b2
        return x + gate_mlp[:, None] * ff_out
    x = _L0_cond_ref(x, cond_1024, mask_BxS_bk0, L0_cond_ada_w, L0_cond_ada_b, L0_cond_ssm_w1, L0_cond_ssm_b1, L0_cond_ssm_w2, L0_cond_ssm_b2, L0_cond_bwd_w1, L0_cond_bwd_b1, L0_cond_bwd_w2, L0_cond_bwd_b2, L0_cond_ffada_w, L0_cond_ffada_b, L0_cond_ff_w1, L0_cond_ff_b1, L0_cond_ff_w2, L0_cond_ff_b2)
    return x

_drawn_inputs = setup_inputs


def setup_inputs(seed=0):
    import zlib

    import numpy as np

    out = dict(_drawn_inputs(seed))
    spreads = {'L0_cond_ada_b': (0.0, 0.8),
     'L0_cond_ssm_b1': (0.0, 0.8),
     'L0_cond_ssm_b2': (0.0, 0.787),
     'L0_cond_bwd_b1': (0.0, 0.8),
     'L0_cond_bwd_b2': (0.0, 0.766),
     'L0_cond_ffada_b': (0.0, 0.374),
     'L0_cond_ff_b1': (0.0, 0.697),
     'L0_cond_ff_b2': (0.0, 0.29)}
    factors = {'L0_cond_ssm_w1': 4.462,
     'L0_cond_ssm_w2': 4.147,
     'L0_cond_bwd_w1': 4.46,
     'L0_cond_bwd_w2': 4.155}
    for name, (base, spread) in spreads.items():
        noise = np.random.default_rng([zlib.crc32(name.encode()), seed]).standard_normal(out[name].shape)
        drawn = base * np.exp(spread * noise) if base else spread * noise
        out[name] = jnp.asarray(drawn.astype(out[name].dtype))
    for name, factor in factors.items():
        out[name] = (out[name] * factor).astype(out[name].dtype)
    return out
```

```python
from contextlib import ExitStack

import concourse.bass as bass
from concourse import mybir

F32 = mybir.dt.float32
F32R = mybir.dt.float32r
U32 = mybir.dt.uint32
I32 = mybir.dt.int32
U8 = mybir.dt.uint8
ALU = mybir.AluOpType
ACT = mybir.ActivationFunctionType
AX = mybir.AxisListType

P = 128
EPS = 1e-6
DMA = 16
FREE = 1


def build(nc, x, cond, mask, ada_w, ada_b, ssm_w1, ssm_b1, ssm_w2, ssm_b2, bwd_w1, bwd_b1, bwd_w2, bwd_b2,
          ffada_w, ffada_b, ff_w1, ff_b1, ff_w2, ff_b2, out):
    B, S, D = x.shape
    T = B * S
    K = D // P
    J = S // P
    HID = ff_w1.shape[1]
    M = HID // P
    C = T // P
    HALF = M // 2
    STEP = P // B
    assert HID == 2 * D and S == D and J == K and STEP * B == P and T < 1 << 23
    NONE = float(8 * T)
    TURN_AFTER = [2, 3, 4, 5]

    ctx = ExitStack()
    with ctx:
        def sb(name, shape, dt=F32):
            return ctx.enter_context(nc.sbuf_tensor(name, shape, dt))

        def sem(name):
            return ctx.enter_context(nc.semaphore(name))

        w1_hi = sb("w1_hi", [P, K, HID], F32R)
        w1_lo = sb("w1_lo", [P, K, HID], F32R)
        w2_hi = sb("w2_hi", [P, M, D], F32R)
        w2_lo = sb("w2_lo", [P, M, D], F32R)
        h_hi = sb("h_hi", [P, M, S], F32R)
        h_lo = sb("h_lo", [P, M, S], F32R)
        y_hi = sb("y_hi", [P, K, S], F32R)
        y_lo = sb("y_lo", [P, K, S], F32R)
        full = sb("full", [P, 4, S])
        xhat = sb("xhat", [P, J, D])
        stage = sb("stage", [P, 3, K, D])
        region = sb("region", [P, 24, 512])
        xg = region[:, 0:4, :]
        tab_ln = region[:, 4:12, :].rearrange("p (j t) d -> p j (t d)", j=J)
        tab_out = region[:, 12:20, :].rearrange("p (j t) d -> p j (t d)", j=J)
        xr = region[:, 20:24, :]
        x_sb = [region[:, 0:4, :], region[:, 4:8, :]]
        gate_sb = [region[:, 8:10, :], region[:, 10:12, :]]
        o_sb = [region[:, 12:16, :], region[:, 16:20, :]]
        raw_w1 = region[:, 0:8, :]
        raw_w2 = region[:, 12:20, :]
        rows_a = region[0:B, 8:12, :]
        bias_a = region[0:B, 20:24, :]
        bias_b = region[0:B, 12:16, :]
        cond_sb = region[0:B, 16, :]
        silu_sb = region[0:B, 17, :]
        b2_bwd = region[0:B, 18, :]
        rows_b = full[0:B, :, :]

        turn = sb("turn", [P, 2 * P])
        ident = turn[:, 0:P]
        siluT = sb("siluT", [P, K, B])
        mod_b = sb("mod_b", [P, B + 1, 2, K])
        mod_cur = sb("mod_cur", [P, 2, 2, K])
        b1_a = sb("b1_a", [P, M])
        b1_b = sb("b1_b", [P, M])
        tok_no = sb("tok_no", [P, C + J], U32)
        row_no = sb("row_no", [P, C + J], U32)
        over_no = sb("over_no", [P, C + J], U32)
        idx_ln = sb("idx_ln", [P, 2, J], U32)
        idx_out = sb("idx_out", [P, 2, J], U32)
        idx_over = sb("idx_over", [P, J], U32)
        mask_u8 = sb("mask_u8", [P, C], U8)
        stats = sb("stats", [P, J, 6])
        mean_var = sb("mean_var", [P, J, 2])
        var_eps = sb("var_eps", [P, J])
        minus_half = sb("minus_half", [P, J])
        rstd = sb("rstd", [P, J])
        runs_f = sb("runs_f", [1, 4])
        runs = sb("runs", [1, 2], I32)
        key = xhat[:, 0, 0:C]
        key_turned = xhat[:, 0, C:2 * C]
        is_masked = xhat[:, 0, 2 * C:3 * C]
        count = xhat[:, 0, 3 * C:4 * C]
        found = xhat[:, 1, 0:C]
        first_no = xhat[:, 1, C:2 * C]
        slot_base = xhat[:, 1, 2 * C:3 * C]
        address = xhat[:, 1, 3 * C:4 * C]
        zeros = xhat[:, 2, 0:C]

        ps_o = [ctx.enter_context(nc.psum_tensor(f"ps_o{j}", [P, 512], F32)) for j in range(J)]
        ps_h = [ctx.enter_context(nc.psum_tensor(f"ps_h{i}", [P, 512], F32)) for i in range(2)]
        ps_x = [ctx.enter_context(nc.psum_tensor(f"ps_x{i}", [P, 512], F32)) for i in range(2)]

        compact = nc.dram_tensor("compact_rows", [T + S, D], F32).ap()
        table_ln = nc.dram_tensor("table_ln", [B, 2 * D], F32).ap()
        table_out = nc.dram_tensor("table_out", [B, 2 * D], F32).ap()
        table_b = nc.dram_tensor("table_b", [B, 2 * D], F32).ap()
        x_rows = x.rearrange("b s d -> (b s) d")
        x_tiles = x.rearrange("b (p j) d -> b p j d", j=J)
        out_tiles = out.rearrange("b (p j) d -> b p j d", j=J)
        compact_blocks = compact.rearrange("(i j p) d -> i p j d", p=P, j=J)


        mask_in, cond_in, bias_in, b1_in = sem("mask_in"), sem("cond_in"), sem("bias_in"), sem("b1_in")
        ada_in = [sem(f"ada_in{i}") for i in range(6)]
        raw_w1_in, raw_w2_in = sem("raw_w1_in"), sem("raw_w2_in")
        ff_w1_in, ff_w2_in = sem("ff_w1_in"), sem("ff_w2_in")
        consts_set = sem("consts_set")
        turn_zero, turn_half, turn_ready = sem("turn_zero"), sem("turn_half"), sem("turn_ready")
        silu_done, cond_turned, siluT_ready = sem("silu_done"), sem("cond_turned"), sem("siluT_ready")
        ada_done = sem("ada_done")
        dve_step = sem("dve_step")
        key_ready, key_turned_ps, address_ready, address_ps = (
            sem("key_ready"), sem("key_turned_ps"), sem("address_ready"), sem("address_ps"))
        most_ps, lists_ready, runs_ready = sem("most_ps"), sem("lists_ready"), sem("runs_ready")
        rows_a_ready, rows_b_ready = sem("rows_a_ready"), sem("rows_b_ready")
        tables_a_out, table_b_out = sem("tables_a_out"), sem("table_b_out")
        mod_ps, mod_ready = sem("mod_ps"), sem("mod_ready")
        w1_hi_ready, w1_lo_ready = sem("w1_hi_ready"), sem("w1_lo_ready")
        w2_hi_ready, w2_lo_ready = sem("w2_hi_ready"), sem("w2_lo_ready")

        class Pipe:

            def __init__(self, tag):
                self.stats_done = sem(f"{tag}_stats_done")
                self.mean_done = sem(f"{tag}_mean_done")
                self.var_ready = sem(f"{tag}_var_ready")
                self.rstd_ready = sem(f"{tag}_rstd_ready")
                self.xhat_ready = sem(f"{tag}_xhat_ready")
                self.x_turned = sem(f"{tag}_x_turned")
                self.y_hi_ready = sem(f"{tag}_y_hi_ready")
                self.y_lo_ready = sem(f"{tag}_y_lo_ready")
                self.h_summed = sem(f"{tag}_h_summed")
                self.h_hi_ready = sem(f"{tag}_h_hi_ready")
                self.h_lo_ready = sem(f"{tag}_h_lo_ready")
                self.o_summed = sem(f"{tag}_o_summed")
                self.gated = sem(f"{tag}_gated")
                self.out_ready = sem(f"{tag}_out_ready")

        a, b = Pipe("a"), Pipe("b")
        a_idx_ln, a_idx_out = sem("a_idx_ln"), sem("a_idx_out")
        a_rows_in, a_res_in = sem("a_rows_in"), sem("a_res_in")
        a_scaled, a_biased = sem("a_scaled"), sem("a_biased")
        a_stored, a_filled = sem("a_stored"), sem("a_filled")
        b_x_in = [sem("b_x_in0"), sem("b_x_in1")]
        b_gate_in = [sem("b_gate_in0"), sem("b_gate_in1")]
        b_idx_over, b_over_in = sem("b_idx_over"), sem("b_over_in")
        b_mod_cur, b_based = sem("b_mod_cur"), sem("b_based")
        waited = sem("waited")
        b_stored = [sem("b_stored0"), sem("b_stored1")]

        block = ctx.enter_context(nc.Block())

        def thirds(w):
            return w.rearrange("(k p) (c n) -> c p k n", p=P, c=3)

        def wait_alone(eng, semaphore, value):
            eng.wait_ge(semaphore, value)
            eng.sem_inc(waited, 1)

        def runs_of(eng):
            eng.wait_ge(runs_ready, 1)
            return eng.value_load(runs[0:1, 0:1], min_val=1, max_val=C // J)

        @block.sync
        def _(sp):
            with nc.allow_non_contiguous_dma(reason="four mask bytes, single biases"):
                sp.dma_start(mask_u8[:, :].rearrange("p (b j) -> p b j", j=J),
                             mask.rearrange("b (p j) -> p b j", j=J)).then_inc(mask_in, DMA)
            for u in range(2):
                sp.sem_inc(b_stored[u], FREE)
            sp.dma_start(cond_sb, cond).then_inc(cond_in, DMA)
            for c in range(3):
                sp.dma_start(stage[:, c, :, :], thirds(ada_w)[c]).then_inc(ada_in[c], DMA)
            for t, (vec, width) in enumerate(((ada_b, 3), (ssm_b2, 1), (bwd_b2, 1), (ffada_b, 3), (ff_b2, 1))):
                to = (bias_a[:, 0:3, :], bias_a[:, 3:4, :], b2_bwd.rearrange("p (o d) -> p o d", o=1),
                      bias_b[:, 0:3, :], bias_b[:, 3:4, :])[t]
                sp.dma_start(to, vec.rearrange("(o w d) -> o w d", o=1, w=width)
                             .to_broadcast([B, width, D])).then_inc(bias_in, DMA)
            raw = raw_w1.rearrange("p (k t) d -> p k t d", k=K)
            sp.dma_start(raw[:, :, 0, :], ssm_w1.rearrange("(k p) n -> p k n", p=P)).then_inc(raw_w1_in, DMA)
            sp.dma_start(raw[:, :, 1, :], bwd_w1.rearrange("(k p) n -> p k n", p=P)).then_inc(raw_w1_in, DMA)
            with nc.allow_non_contiguous_dma(reason="four mask bytes, single biases"):
                sp.dma_start(b1_a[:, 0:HALF], ssm_b1.rearrange("(m p) -> p m", p=P)).then_inc(b1_in, DMA)
                sp.dma_start(b1_a[:, HALF:M], bwd_b1.rearrange("(m p) -> p m", p=P)).then_inc(b1_in, DMA)
                sp.dma_start(b1_b[:, :], ff_b1.rearrange("(m p) -> p m", p=P)).then_inc(b1_in, DMA)
            for c in range(3):
                sp.wait_ge(ada_done, c + 1)
                sp.dma_start(stage[:, c, :, :], thirds(ffada_w)[c]).then_inc(ada_in[3 + c], DMA)
            sp.wait_ge(rows_a_ready, 1)
            sp.dma_start(table_ln.rearrange("b (t d) -> b t d", t=2), rows_a[:, 0:2, :]).then_inc(tables_a_out, DMA)
            sp.dma_start(table_out.rearrange("b (t d) -> b t d", t=2), rows_a[:, 2:4, :]).then_inc(tables_a_out, DMA)
            sp.wait_ge(rows_b_ready, 1)
            sp.dma_start(table_b.rearrange("b (t d) -> b t d", t=2), rows_b[:, 2:4, :]).then_inc(table_b_out, DMA)
            sp.dma_start(raw_w2[:, 0:HALF, :], ssm_w2.rearrange("(m p) n -> p m n", p=P)).then_inc(raw_w2_in, DMA)
            sp.dma_start(raw_w2[:, HALF:M, :], bwd_w2.rearrange("(m p) n -> p m n", p=P)).then_inc(raw_w2_in, DMA)
            sp.wait_ge(ada_done, 6)
            stage_raw = stage[:, 0:2, :, :].rearrange("p c k d -> p (c k d)")
            sp.dma_start(stage_raw.rearrange("p (k n) -> p k n", k=K),
                         ff_w1.rearrange("(k p) n -> p k n", p=P)).then_inc(ff_w1_in, DMA)

            n = runs_of(sp)
            with sp.Fori(n, C // J + 1) as i:
                sp.dma_start(compact_blocks[bass.ds(i, 1)].rearrange("o p j d -> (o p) j d"), stage[:, 2, :, :]
                             ).then_inc(a_filled, DMA)

            def load_row(s, u):
                sp.dma_start(x_sb[u], x_tiles[bass.ds(s, 1)].rearrange("o p j d -> (o p) j d")
                             ).then_inc(b_x_in[u], DMA)
                sp.dma_start(gate_sb[u], table_b[bass.ds(s, 1), :].rearrange("o (t d) -> o t d", t=2)
                             .to_broadcast([P, 2, D])).then_inc(b_gate_in[u], DMA)

            sp.wait_ge(table_b_out, DMA)
            sp.wait_ge(a.xhat_ready, J * n + J)
            load_row(0, 0)
            sp.wait_ge(w1_hi_ready, 2)
            sp.wait_ge(w1_lo_ready, 2)
            sp.dma_start(stage_raw.rearrange("p (m n) -> p m n", m=M),
                         ff_w2.rearrange("(m p) n -> p m n", p=P)).then_inc(ff_w2_in, DMA)
            load_row(1, 1)
            with sp.Fori(0, B // 2) as i:
                for u in range(2):
                    s = 2 * i + u
                    sp.wait_ge(b.out_ready, J * s + J)
                    sp.dma_start(out_tiles[bass.ds(s, 1)].rearrange("o p j d -> (o p) j d"), o_sb[u]
                                 ).then_inc(b_stored[u], DMA)
                    load_row((s + 2) % B, u)
            for u in range(2):
                sp.wait_ge(b_stored[u], DMA * (B // 2) + FREE)
                sp.wait_ge(b_x_in[u], DMA * (B // 2 + 1))
                sp.wait_ge(b_gate_in[u], DMA * (B // 2 + 1))

        @block.gpsimd
        def _(pool):
            nc.gpsimd.memset(turn[:, :], 0.0).then_inc(turn_zero, 1)
            nc.gpsimd.memset(minus_half[:, :], -0.5).then_inc(consts_set, 1)
            pool.wait_ge(turn_zero, 1)
            nc.gpsimd.affine_select(out=turn[:, 0:P], in_=turn[:, 0:P], compare_op=ALU.not_equal, fill=1.0, base=0,
                                    pattern=[[-1, P]], channel_multiplier=1).then_inc(turn_ready, 1)
            nc.gpsimd.affine_select(out=turn[:, P:2 * P], in_=turn[:, P:2 * P], compare_op=ALU.not_equal, fill=1.0,
                                    base=0, pattern=[[-1, P]], channel_multiplier=1).then_inc(turn_ready, 1)
            nc.gpsimd.iota(first_no.rearrange("p (b j) -> p b j", j=J), pattern=[[-S, B], [-1, J]], base=T,
                           channel_multiplier=-J, allow_small_or_imprecise_dtypes=True).then_inc(consts_set, 1)
            nc.gpsimd.iota(slot_base, pattern=[[0, C]], base=-P, channel_multiplier=1,
                           allow_small_or_imprecise_dtypes=True).then_inc(consts_set, 1)

            def power(pipe, t):
                pool.wait_ge(pipe.var_ready, t + 1)
                nc.gpsimd.tensor_tensor(out=rstd[:, :], in0=var_eps[:, :], in1=minus_half[:, :],
                                        op=ALU.pow).then_inc(pipe.rstd_ready, 1)

            def gather(to, table, index, done):
                nc.gpsimd.indirect_dma_start(out=to, out_offset=None, in_=table,
                                             in_offset=bass.IndirectOffsetOnAxis(ap=index, axis=0)).then_inc(done, DMA)

            def gather_rows(t):
                wait_alone(pool, a_idx_ln, t + 1)
                for j in range(J):
                    gather(xg[:, j, :], x_rows, idx_ln[:, 0, j:j + 1], a_rows_in)
                for j in range(J):
                    gather(tab_ln[:, j, :], table_ln, idx_ln[:, 1, j:j + 1], a_rows_in)

            pool.wait_ge(tables_a_out, 2 * DMA)
            pool.wait_ge(w1_hi_ready, 1)
            pool.wait_ge(w1_lo_ready, 1)
            gather_rows(0)
            power(a, 0)
            pool.wait_ge(w2_hi_ready, 1)
            pool.wait_ge(w2_lo_ready, 1)
            n = runs_of(pool)
            with pool.Fori(0, n) as i:
                wait_alone(pool, a_idx_out, i + 1)
                for j in range(J):
                    gather(tab_out[:, j, :], table_out, idx_out[:, 1, j:j + 1], a_res_in)
                for j in range(J):
                    gather(xr[:, j, :], x_rows, idx_out[:, 0, j:j + 1], a_res_in)
                gather_rows(i + 1)
                power(a, i + 1)
                wait_alone(pool, a.out_ready, J * i + J)
                pool.dma_start(compact_blocks[bass.ds(i, 1)].rearrange("o p j d -> (o p) j d"), xr
                               ).then_inc(a_stored, DMA)
                wait_alone(pool, a_stored, DMA * i + DMA)

            def overlay(u, loads):
                wait_alone(pool, b_x_in[u], DMA * loads)
                for j in range(J):
                    nc.gpsimd.indirect_dma_start(
                        out=x_sb[u][:, j, :], out_offset=None, in_=compact,
                        in_offset=bass.IndirectOffsetOnAxis(ap=idx_over[:, j:j + 1], axis=0),
                        bounds_check=T + S - 1, oob_is_err=False).then_inc(b_over_in, DMA)

            fills = pool.value_load(runs[0:1, 1:2], min_val=1, max_val=C // J)
            wait_alone(pool, a_filled, DMA * fills)
            pool.wait_ge(b_idx_over, 1)
            overlay(0, 1)
            power(b, 0)
            with pool.Fori(0, B // 2) as i:
                for u in range(2):
                    s = 2 * i + u
                    pool.wait_ge(b_idx_over, s + 2)
                    overlay(1 - u, i + 1 + u)
                    power(b, s + 1)

        @block.scalar
        def _(act):
            act.wait_ge(cond_in, DMA)
            nc.scalar.activation(silu_sb, cond_sb, ACT.Silu).then_inc(silu_done, 1)
            act.wait_ge(raw_w1_in, 2 * DMA)
            nc.scalar.activation(w1_hi[:, :, :].rearrange("p k n -> p (k n)"), raw_w1.rearrange("p t d -> p (t d)"),
                                 ACT.Copy).then_inc(w1_hi_ready, 1)

            def cut_hidden(pipe, s, b1, func):
                for m in range(M):
                    act.wait_ge(pipe.h_summed, M * s + m + 1)
                    if m >= 2:
                        act.wait_ge(pipe.h_lo_ready, M * s + m - 1)
                    nc.scalar.activation(full[:, m % 2, :], ps_h[m % 2][:, :], func, bias=b1[:, m:m + 1])
                    nc.scalar.activation(h_hi[:, m, :], ps_h[m % 2][:, :], func,
                                         bias=b1[:, m:m + 1]).then_inc(pipe.h_hi_ready, 1)

            def cut_input(pipe, t, u):
                for k in range(K):
                    act.wait_ge(pipe.x_turned, K * t + k + 1)
                    if k >= 2:
                        act.wait_ge(pipe.y_lo_ready, K * t + k - 1)
                    for to in (full[:, 2 + k % 2, :], y_hi[:, k, :]):
                        if u is None:
                            last = nc.scalar.activation(to, ps_x[k % 2][:, :], ACT.Copy)
                        else:
                            last = nc.scalar.activation(to, ps_x[k % 2][:, :], ACT.Identity,
                                                        scale=mod_cur[:, u, 0, k:k + 1], bias=mod_cur[:, u, 1, k:k + 1])
                    last.then_inc(pipe.y_hi_ready, 1)

            act.wait_ge(table_b_out, DMA)
            cut_input(a, 0, None)
            act.wait_ge(raw_w2_in, 2 * DMA)
            nc.scalar.activation(w2_hi[:, :, :].rearrange("p k n -> p (k n)"), raw_w2.rearrange("p t d -> p (t d)"),
                                 ACT.Copy).then_inc(w2_hi_ready, 1)
            act.wait_ge(b1_in, 3 * DMA)
            n = runs_of(act)
            with act.Fori(0, n) as i:
                cut_hidden(a, i, b1_a, ACT.Gelu)
                cut_input(a, i + 1, None)

            act.wait_ge(a.o_summed, n)
            act.wait_ge(ff_w1_in, DMA)
            raw = stage[:, 0:2, :, :].rearrange("p c k d -> p (c k d)")
            nc.scalar.activation(w1_hi[:, :, :].rearrange("p k n -> p (k n)"), raw, ACT.Copy).then_inc(w1_hi_ready, 1)
            act.wait_ge(b_mod_cur, 1)
            cut_input(b, 0, 0)
            act.wait_ge(ff_w2_in, DMA)
            nc.scalar.activation(w2_hi[:, :, :].rearrange("p k n -> p (k n)"), raw, ACT.Copy).then_inc(w2_hi_ready, 1)
            with act.Fori(0, B // 2) as i:
                for u in range(2):
                    s = 2 * i + u
                    cut_hidden(b, s, b1_b, ACT.Gelu_apprx_tanh)
                    act.wait_ge(b_mod_cur, s + 2)
                    cut_input(b, s + 1, 1 - u)

        @block.vector
        def _(dve):
            steps = [0]

            def link(ins):
                steps[0] += 1
                ins.then_inc(dve_step, 1)
                dve.wait_ge(dve_step, steps[0])

            dve.sem_inc(a.gated, FREE)
            dve.sem_inc(b.gated, FREE)

            dve.wait_ge(mask_in, DMA)
            dve.wait_ge(consts_set, 3)
            nc.vector.memset(zeros, 0.0)
            link(nc.vector.tensor_copy(found, mask_u8[:, :]))
            nc.vector.tensor_tensor(key, found, first_no, ALU.mult).then_inc(key_ready, 1)
            dve.wait_ge(key_turned_ps, 1)
            link(nc.vector.tensor_copy(key_turned, ps_h[0][:, 0:C]))
            link(nc.vector.tensor_scalar(is_masked, key_turned, 0.0, None, ALU.is_gt))
            link(nc.vector.tensor_tensor_scan(count, is_masked, zeros, 0.0, ALU.add, ALU.add))
            link(nc.vector.scalar_tensor_tensor(out=address, in0=count, scalar=float(P), in1=slot_base,
                                                op0=ALU.mult, op1=ALU.add))
            link(nc.vector.tensor_scalar(address, address, NONE, None, ALU.subtract))
            link(nc.vector.tensor_tensor(address, address, is_masked, ALU.mult))
            nc.vector.tensor_scalar(address, address, NONE, None, ALU.add).then_inc(address_ready, 1)
            for r in range(C // 8):
                link(nc.vector.max(found[:, 8 * r:8 * r + 8], key_turned))
                link(nc.vector.match_replace(key_turned, found[:, 8 * r:8 * r + 8], key_turned, 0.0))
            link(nc.vector.tensor_scalar(found, found, -1.0, float(T), ALU.mult, ALU.add))
            link(nc.vector.tensor_scalar(tok_no[:, 0:C], found, float(T - 1), None, ALU.min))
            link(nc.vector.memset(tok_no[:, C:C + J], 0))
            link(nc.vector.tensor_scalar(row_no[:, :], tok_no[:, :], S.bit_length() - 1, None, ALU.logical_shift_right))
            dve.wait_ge(address_ps, 1)
            link(nc.vector.tensor_copy(over_no[:, 0:C], ps_h[1][:, 0:C]))
            link(nc.vector.memset(over_no[:, C:C + J], int(NONE)))
            dve.wait_ge(most_ps, 1)
            link(nc.vector.tensor_reduce(runs_f[0:1, 0:1], ps_x[1][0:1, 0:P], AX.X, ALU.max))
            link(nc.vector.tensor_scalar(runs_f[0:1, 1:2], runs_f[0:1, 0:1], 1.0, float(J - 1), ALU.max, ALU.add))
            link(nc.vector.tensor_scalar(runs_f[0:1, 2:3], runs_f[0:1, 1:2], 1.0 / J, -(J - 1) / (2.0 * J),
                                         ALU.mult, ALU.add))
            link(nc.vector.tensor_copy(runs[0:1, 0:1], runs_f[0:1, 2:3]))
            nc.vector.tensor_scalar(runs[0:1, 1:2], runs[0:1, 0:1], -1.0, float(C // J + 1),
                                    ALU.mult, ALU.add).then_inc(runs_ready, 1)

            dve.wait_ge(cond_turned, 1)
            nc.vector.tensor_copy(siluT[:, :, :].rearrange("p k b -> p (k b)"),
                                  ps_x[0][:, 0:K * B]).then_inc(siluT_ready, 1)
            dve.wait_ge(bias_in, 5 * DMA)
            link(nc.vector.tensor_tensor(b2_bwd, b2_bwd, bias_a[:, 3, :], ALU.add))

            def modulation(first, rows, bias, b2):
                for c, to in enumerate((1, 0, 2)):
                    dve.wait_ge(ada_done, first + c + 1)
                    link(nc.vector.tensor_tensor(rows[:, to, :], ps_o[c][0:B, :], bias[:, c, :], ALU.add))
                link(nc.vector.tensor_scalar(rows[:, 0, :], rows[:, 0, :], 1.0, None, ALU.add))
                return nc.vector.tensor_tensor(rows[:, 3, :], rows[:, 2, :], b2, ALU.mult)

            modulation(0, rows_a, bias_a, b2_bwd).then_inc(rows_a_ready, 1)

            def copy_numbers(to, t):
                nc.vector.tensor_copy(to[:, 0, :], tok_no[:, bass.ds(J * t, J)])
                return nc.vector.tensor_copy(to[:, 1, :], row_no[:, bass.ds(J * t, J)])

            copy_numbers(idx_ln, 0).then_inc(a_idx_ln, 1)

            dve.wait_ge(w1_hi_ready, 1)
            nc.vector.tensor_tensor(w1_lo[:, :, :].rearrange("p k n -> p (k n)"), raw_w1.rearrange("p t d -> p (t d)"),
                                    w1_hi[:, :, :].rearrange("p k n -> p (k n)").bitcast(F32),
                                    ALU.subtract).then_inc(w1_lo_ready, 1)
            modulation(3, rows_b, bias_b, bias_b[:, 3, :]).then_inc(rows_b_ready, 1)
            dve.wait_ge(mod_ps, 1)
            nc.vector.tensor_copy(mod_b[:, 0:B, :, :].rearrange("p b t k -> p t k b"),
                                  ps_h[0][:, 0:2 * K * B].rearrange("p (t k b) -> p t k b", t=2, k=K)
                                  ).then_inc(mod_ready, 1)
            link(nc.vector.memset(mod_b[:, B, :, :], 0.0))

            def statistics(pipe, t, tokens):
                for j in range(J):
                    nc.vector.bn_stats(stats[:, j, :], tokens[:, j, :]).then_inc(pipe.stats_done, 1)
                wait_alone(dve, pipe.stats_done, J * t + J)
                for j in range(J):
                    nc.vector.bn_aggr(mean_var[:, j, :], stats[:, j, :]).then_inc(pipe.mean_done, 1)
                dve.wait_ge(pipe.mean_done, J * t + J)
                nc.vector.tensor_scalar(var_eps[:, :], mean_var[:, :, 1], EPS, None, ALU.add).then_inc(pipe.var_ready, 1)

            def normal(j, tokens):
                return nc.vector.tensor_scalar(xhat[:, j, :], tokens[:, j, :], mean_var[:, j, 0:1], rstd[:, j:j + 1],
                                               ALU.subtract, ALU.mult)

            def low_input(pipe, t):
                for k in range(K):
                    dve.wait_ge(pipe.y_hi_ready, K * t + k + 1)
                    nc.vector.tensor_tensor(y_lo[:, k, :], full[:, 2 + k % 2, :], y_hi[:, k, :].bitcast(F32),
                                            ALU.subtract).then_inc(pipe.y_lo_ready, 1)

            def low_hidden(pipe, s):
                for m in range(M):
                    dve.wait_ge(pipe.h_hi_ready, M * s + m + 1)
                    nc.vector.tensor_tensor(h_lo[:, m, :], full[:, m % 2, :], h_hi[:, m, :].bitcast(F32),
                                            ALU.subtract).then_inc(pipe.h_lo_ready, 1)

            def normalise_a(t):
                dve.wait_ge(a_rows_in, 2 * J * DMA * t + 2 * J * DMA)
                statistics(a, t, xg)
                dve.wait_ge(a.rstd_ready, t + 1)
                for j in range(J):
                    normal(j, xg).then_inc(a_scaled, 1)
                for j in range(J):
                    dve.wait_ge(a_scaled, 2 * J * t + j + 1)
                    nc.vector.tensor_tensor(xhat[:, j, :], xhat[:, j, :], tab_ln[:, j, 0:D],
                                            ALU.mult).then_inc(a_scaled, 1)
                for j in range(J):
                    dve.wait_ge(a_scaled, 2 * J * t + J + j + 1)
                    nc.vector.tensor_tensor(xhat[:, j, :], xhat[:, j, :], tab_ln[:, j, D:2 * D],
                                            ALU.add).then_inc(a.xhat_ready, 1)

            normalise_a(0)
            low_input(a, 0)
            dve.wait_ge(w2_hi_ready, 1)
            nc.vector.tensor_tensor(w2_lo[:, :, :].rearrange("p k n -> p (k n)"), raw_w2.rearrange("p t d -> p (t d)"),
                                    w2_hi[:, :, :].rearrange("p k n -> p (k n)").bitcast(F32),
                                    ALU.subtract).then_inc(w2_lo_ready, 1)
            n = runs_of(dve)
            with dve.Fori(0, n) as i:
                copy_numbers(idx_out, i).then_inc(a_idx_out, 1)
                copy_numbers(idx_ln, i + 1).then_inc(a_idx_ln, 1)
                low_hidden(a, i)
                normalise_a(i + 1)
                low_input(a, i + 1)
                dve.wait_ge(a_res_in, 2 * J * DMA * i + 2 * J * DMA)
                dve.wait_ge(a.o_summed, i + 1)
                for j in range(J):
                    nc.vector.tensor_tensor(tab_out[:, j, 0:D], ps_o[j][:, :], tab_out[:, j, 0:D],
                                            ALU.mult).then_inc(a.gated, 1)
                for j in range(J):
                    nc.vector.tensor_tensor(xr[:, j, :], xr[:, j, :], tab_out[:, j, D:2 * D],
                                            ALU.add).then_inc(a_biased, 1)
                for j in range(J):
                    dve.wait_ge(a.gated, J * i + j + 1 + FREE)
                    dve.wait_ge(a_biased, J * i + j + 1)
                    nc.vector.tensor_tensor(xr[:, j, :], xr[:, j, :], tab_out[:, j, 0:D],
                                            ALU.add).then_inc(a.out_ready, 1)

            def copy_current(t, u):
                nc.vector.tensor_copy(idx_over[:, :], over_no[:, bass.ds(J * t, J)]).then_inc(b_idx_over, 1)
                nc.vector.tensor_copy(mod_cur[:, u, :, :], mod_b[:, bass.ds(t, 1), :, :].rearrange(
                    "p o t k -> p (o t) k")).then_inc(b_mod_cur, 1)

            def normalise_b(t, u, in_count):
                dve.wait_ge(b_over_in, J * DMA * t + J * DMA)
                dve.wait_ge(b_gate_in[u], in_count)
                statistics(b, t, x_sb[u])
                dve.wait_ge(b.rstd_ready, t + 1)
                for j in range(J):
                    normal(j, x_sb[u]).then_inc(b.xhat_ready, 1)
                for j in range(J):
                    nc.vector.tensor_tensor(x_sb[u][:, j, :], x_sb[u][:, j, :], gate_sb[u][:, 1, :],
                                            ALU.add).then_inc(b_based, 1)

            copy_current(0, 0)
            dve.wait_ge(w1_hi_ready, 2)
            raw = stage[:, 0:2, :, :].rearrange("p c k d -> p (c k d)")
            nc.vector.tensor_tensor(w1_lo[:, :, :].rearrange("p k n -> p (k n)"), raw,
                                    w1_hi[:, :, :].rearrange("p k n -> p (k n)").bitcast(F32),
                                    ALU.subtract).then_inc(w1_lo_ready, 1)
            normalise_b(0, 0, DMA)
            low_input(b, 0)
            dve.wait_ge(w2_hi_ready, 2)
            nc.vector.tensor_tensor(w2_lo[:, :, :].rearrange("p k n -> p (k n)"), raw,
                                    w2_hi[:, :, :].rearrange("p k n -> p (k n)").bitcast(F32),
                                    ALU.subtract).then_inc(w2_lo_ready, 1)
            with dve.Fori(0, B // 2) as i:
                for u in range(2):
                    s = 2 * i + u
                    copy_current(s + 1, 1 - u)
                    low_hidden(b, s)
                    normalise_b(s + 1, 1 - u, DMA * (i + 1) + DMA * u)
                    low_input(b, s + 1)
                    dve.wait_ge(b_stored[u], DMA * i + FREE)
                    dve.wait_ge(b.o_summed, s + 1)
                    for j in range(J):
                        nc.vector.tensor_tensor(o_sb[u][:, j, :], ps_o[j][:, :], gate_sb[u][:, 0, :],
                                                ALU.mult).then_inc(b.gated, 1)
                    for j in range(J):
                        dve.wait_ge(b.gated, J * s + j + 1 + FREE)
                        nc.vector.tensor_tensor(o_sb[u][:, j, :], o_sb[u][:, j, :], x_sb[u][:, j, :],
                                                ALU.add).then_inc(b.out_ready, 1)

        @block.tensor
        def _(pe):
            pe.wait_ge(turn_ready, 2)
            pe.wait_ge(key_ready, 1)
            for r in range(B):
                last = nc.tensor.matmul(ps_h[0][:, J * r:J * r + J], turn[:, P - STEP * r:2 * P - STEP * r],
                                        key[:, J * r:J * r + J], start=True, stop=True)
            last.then_inc(key_turned_ps, 1)
            pe.wait_ge(silu_done, 1)
            for k in range(K):
                last = nc.tensor.transpose(ps_x[0][:, B * k:B * k + B], silu_sb[:, P * k:P * k + P], ident[0:B, 0:B])
            last.then_inc(cond_turned, 1)
            pe.wait_ge(address_ready, 1)
            nc.tensor.transpose(ps_x[1][0:1, 0:P], count[:, C - 1:C], ident).then_inc(most_ps, 1)
            for r in range(B):
                last = nc.tensor.matmul(ps_h[1][:, J * r:J * r + J], turn[:, STEP * r:STEP * r + P],
                                        address[:, J * r:J * r + J], start=True, stop=True)
            last.then_inc(address_ps, 1)

            def modulation(first):
                for c in range(3):
                    pe.wait_ge(ada_in[first + c], DMA)
                    for k in range(K):
                        last = nc.tensor.matmul(ps_o[c][0:B, :], siluT[:, k, :], stage[:, c, k, :],
                                                start=(k == 0), stop=(k == K - 1))
                    last.then_inc(ada_done, 1)

            pe.wait_ge(siluT_ready, 1)
            modulation(0)
            pe.wait_ge(rows_a_ready, 1)
            modulation(3)
            pe.wait_ge(rows_b_ready, 1)
            for c in range(2):
                for k in range(K):
                    last = nc.tensor.transpose(ps_h[0][:, (c * K + k) * B:(c * K + k + 1) * B],
                                               rows_b[:, c, P * k:P * k + P], ident[0:B, 0:B])
            last.then_inc(mod_ps, 1)
            pe.wait_ge(mod_ready, 1)

            def turn_chunk(pipe, t, k):
                if k == 0:
                    pe.wait_ge(pipe.xhat_ready, J * t + J)
                if k >= 2:
                    pe.wait_ge(pipe.y_hi_ready, K * t + k - 1)
                for j in range(J):
                    last = nc.tensor.transpose(ps_x[k % 2][:, P * j:P * j + P], xhat[:, j, P * k:P * k + P], ident)
                last.then_inc(pipe.x_turned, 1)

            def layer1(pipe, s):
                for m in range(M):
                    if m >= 2:
                        pe.wait_ge(pipe.h_hi_ready, M * s + m - 1)
                    for k in range(K):
                        if m == 0:
                            pe.wait_ge(pipe.y_hi_ready, K * s + k + 1)
                            pe.wait_ge(pipe.y_lo_ready, K * s + k + 1)
                        w_hi, w_lo = w1_hi[:, k, P * m:P * m + P], w1_lo[:, k, P * m:P * m + P]
                        nc.tensor.matmul(ps_h[m % 2][:, :], w_hi, y_hi[:, k, :], start=(k == 0), stop=False)
                        nc.tensor.matmul(ps_h[m % 2][:, :], w_hi, y_lo[:, k, :], start=False, stop=False)
                        last = nc.tensor.matmul(ps_h[m % 2][:, :], w_lo, y_hi[:, k, :], start=False, stop=(k == K - 1))
                    last.then_inc(pipe.h_summed, 1)

            def layer2(pipe, s):
                pe.wait_ge(pipe.gated, J * s + FREE)
                for m in range(M):
                    pe.wait_ge(pipe.h_hi_ready, M * s + m + 1)
                    pe.wait_ge(pipe.h_lo_ready, M * s + m + 1)
                    for j in range(J):
                        hi, lo = h_hi[:, m, P * j:P * j + P], h_lo[:, m, P * j:P * j + P]
                        nc.tensor.matmul(ps_o[j][:, :], hi, w2_hi[:, m, :], start=(m == 0), stop=False)
                        nc.tensor.matmul(ps_o[j][:, :], hi, w2_lo[:, m, :], start=False, stop=False)
                        last = nc.tensor.matmul(ps_o[j][:, :], lo, w2_hi[:, m, :], start=False, stop=(m == M - 1))
                    if m == M - 1:
                        last.then_inc(pipe.o_summed, 1)
                    if m in TURN_AFTER:
                        turn_chunk(pipe, s + 1, TURN_AFTER.index(m))

            for k in range(K):
                turn_chunk(a, 0, k)
            pe.wait_ge(w1_hi_ready, 1)
            pe.wait_ge(w1_lo_ready, 1)
            pe.wait_ge(w2_hi_ready, 1)
            pe.wait_ge(w2_lo_ready, 1)
            n = runs_of(pe)
            with pe.Fori(0, n) as i:
                layer1(a, i)
                layer2(a, i)
            for k in range(K):
                turn_chunk(b, 0, k)
            wait_alone(pe, a.gated, J * n + FREE)
            pe.wait_ge(w1_hi_ready, 2)
            pe.wait_ge(w1_lo_ready, 2)
            pe.wait_ge(w2_hi_ready, 2)
            pe.wait_ge(w2_lo_ready, 2)
            with pe.Fori(0, B // 2) as i:
                for u in range(2):
                    layer1(b, 2 * i + u)
                    layer2(b, 2 * i + u)


_INS = ['x', 'cond_1024', 'mask_BxS_bk0', 'L0_cond_ada_w', 'L0_cond_ada_b', 'L0_cond_ssm_w1', 'L0_cond_ssm_b1',
        'L0_cond_ssm_w2', 'L0_cond_ssm_b2', 'L0_cond_bwd_w1', 'L0_cond_bwd_b1', 'L0_cond_bwd_w2', 'L0_cond_bwd_b2',
        'L0_cond_ffada_w', 'L0_cond_ffada_b', 'L0_cond_ff_w1', 'L0_cond_ff_b1', 'L0_cond_ff_w2', 'L0_cond_ff_b2']


def kernel(**inputs):
    import numpy as _np
    import concourse.bacc as _bacc
    from concourse import mybir as _mybir
    from concourse.bass_utils import run_bass_kernel_spmd as _run

    nc = _bacc.Bacc("TRN2", target_bir_lowering=False, num_devices=1)
    arrays, args = {}, []
    for name in _INS:
        a = _np.ascontiguousarray(inputs[name])
        arrays[f"in_{name}"] = a
        args.append(nc.dram_tensor(f"in_{name}", a.shape, _mybir.dt.from_np(a.dtype), kind="ExternalInput").ap())
    shape = inputs['x'].shape
    args.append(nc.dram_tensor("out_0", shape, _mybir.dt.float32, kind="ExternalOutput").ap())
    build(nc, *args)
    r = _run(nc, [arrays], core_ids=[0])
    return r.results[0]["out_0"]
```

```python
from contextlib import ExitStack

import concourse.bass as bass
from concourse import mybir

F32 = mybir.dt.float32
BF16 = mybir.dt.bfloat16
F32R = mybir.dt.float32r
U32 = mybir.dt.uint32
I32 = mybir.dt.int32
U8 = mybir.dt.uint8
ALU = mybir.AluOpType
ACT = mybir.ActivationFunctionType
AX = mybir.AxisListType

P = 128
EPS = 1e-6
DMA = 16
FREE = 1


def build(nc, x, cond, mask, ada_w, ada_b, ssm_w1, ssm_b1, ssm_w2, ssm_b2, bwd_w1, bwd_b1, bwd_w2, bwd_b2,
          ffada_w, ffada_b, ff_w1, ff_b1, ff_w2, ff_b2, out):
    B, S, D = x.shape
    T = B * S
    K = D // P
    J = S // P
    HID = ff_w1.shape[1]
    M = HID // P
    C = T // P
    HALF = M // 2
    FEW = 8
    assert HID == 2 * D and S == D and J == K and J * B == P == C and T < 1 << 23 and FEW < C // J
    NONE = float(8 * T)
    TURN_AFTER = [2, 3, 4, 5]

    ctx = ExitStack()
    with ctx:
        def sb(name, shape, dt=F32):
            return ctx.enter_context(nc.sbuf_tensor(name, shape, dt))

        def sem(name):
            return ctx.enter_context(nc.semaphore(name))

        w1_hi = sb("w1_hi", [P, K, HID], F32R)
        w1_lo = sb("w1_lo", [P, K, HID], F32R)
        w2_hi = sb("w2_hi", [P, M, D], F32R)
        w2_lo = sb("w2_lo", [P, M, D], F32R)
        h_hi = sb("h_hi", [P, M, S], F32R)
        h_lo = sb("h_lo", [P, M, S], F32R)
        y_hi = sb("y_hi", [P, K, S], F32R)
        y_lo = sb("y_lo", [P, K, S], F32R)
        full = sb("full", [P, 4, S])
        xhat = sb("xhat", [P, J, D])
        stage = sb("stage", [P, 3, K, D])
        stage_raw = stage[:, 0:2, :, :].rearrange("p c k d -> p (c k d)")
        region = sb("region", [P, 24, 512])
        xg = region[:, 0:4, :]
        tab_ln = region[:, 4:12, :].rearrange("p (j t) d -> p j (t d)", j=J)
        tab_out = region[:, 12:20, :].rearrange("p (j t) d -> p j (t d)", j=J)
        xr = region[:, 20:24, :]
        x_sb = [region[:, 0:4, :], region[:, 4:8, :]]
        gate_sb = [region[:, 8:10, :], region[:, 10:12, :]]
        o_sb = [region[:, 12:16, :], region[:, 16:20, :]]
        cond_sb = region[0:B, 4, :]
        silu_sb = region[0:B, 5, :]
        b2_bwd = region[0:B, 6, :]
        rows_a = region[0:B, 8:12, :]
        raw_w1 = region[:, 12:20, :]
        rows_b = region[0:B, 20:22, :]
        siluT = region[:, 22, 0:K * B].rearrange("p (k b) -> p k b", k=K)
        diff = region[:, 23, 0:P]
        halves = region[:, 23, P:3 * P].bitcast(BF16)
        before = halves[:, 0:P]
        totals_before = halves[:, P:2 * P]

        ident = sb("ident", [P, P])[:, :]
        upto = sb("upto", [P, P], BF16)
        ones = sb("ones", [P, P], BF16)
        mask_bf = sb("mask_bf", [P, C], BF16)
        totals = sb("totals", [P, P], BF16)
        total = sb("total", [P, 1])
        finder = sb("finder", [P, P])
        col_no = sb("col_no", [P, 1])
        col_bits = sb("col_bits", [P, 3], U32)
        edges = sb("edges", [P, 2])
        slot_no = sb("slot_no", [P, S])
        slots = sb("slots", [P, J])
        place = sb("place", [P, J])
        mod_b = sb("mod_b", [P, B + 1, 2, K])
        mod_cur = sb("mod_cur", [P, 2, 2, K])
        b1_a = sb("b1_a", [P, M])
        b1_b = sb("b1_b", [P, M])
        mod_bias = sb("mod_bias", [P, 2, K])
        tok_no = sb("tok_no", [P, C + J], U32)
        row_no = sb("row_no", [P, C + J], U32)
        over_no = sb("over_no", [P, C + J], U32)
        idx_ln = sb("idx_ln", [P, 2, J], U32)
        idx_out = sb("idx_out", [P, 2, J], U32)
        idx_over = sb("idx_over", [P, J], U32)
        mask_u8 = sb("mask_u8", [P, C], U8)
        stats = sb("stats", [P, J, 6])
        mean_var = sb("mean_var", [P, J, 2])
        var_eps = sb("var_eps", [P, J])
        minus_half = sb("minus_half", [P, J])
        rstd = sb("rstd", [P, J])
        runs_f = sb("runs_f", [1, 6])
        runs = sb("runs", [1, 4], I32)
        is_none = full[:, 1, 0:C]

        ps_o = [ctx.enter_context(nc.psum_tensor(f"ps_o{j}", [P, 512], F32)) for j in range(J)]
        ps_h = [ctx.enter_context(nc.psum_tensor(f"ps_h{i}", [P, 512], F32)) for i in range(2)]
        ps_x = [ctx.enter_context(nc.psum_tensor(f"ps_x{i}", [P, 512], F32)) for i in range(2)]

        compact = nc.dram_tensor("compact_rows", [T + S, D], F32).ap()
        table_ln = nc.dram_tensor("table_ln", [B, 2 * D], F32).ap()
        table_out = nc.dram_tensor("table_out", [B, 2 * D], F32).ap()
        table_b = nc.dram_tensor("table_b", [B, 2 * D], F32).ap()
        x_rows = x.rearrange("b s d -> (b s) d")
        x_tiles = x.rearrange("b (p j) d -> b p j d", j=J)
        out_tiles = out.rearrange("b (p j) d -> b p j d", j=J)
        compact_blocks = compact.rearrange("(i j p) d -> i p j d", p=P, j=J)


        mask_in, cond_in, bias_in, b1_in = sem("mask_in"), sem("cond_in"), sem("bias_in"), sem("b1_in")
        ada_in = [sem(f"ada_in{i}") for i in range(6)]
        raw_w1_in, raw_w2_in = sem("raw_w1_in"), sem("raw_w2_in")
        ff_w1_in, ff_w2_in = sem("ff_w1_in"), sem("ff_w2_in")
        consts_set, zeros_set, ident_ready = sem("consts_set"), sem("zeros_set"), sem("ident_ready")
        silu_done, cond_turned, siluT_ready = sem("silu_done"), sem("cond_turned"), sem("siluT_ready")
        ada_done = sem("ada_done")
        dve_step = sem("dve_step")
        mask_ready, totals_ps, totals_ready, ranks_ps = (
            sem("mask_ready"), sem("totals_ps"), sem("totals_ready"), sem("ranks_ps"))
        slot_cols, places_ps, places_read = sem("slot_cols"), sem("places_ps"), sem("places_read")
        runs_ready = sem("runs_ready")
        rows_a_ready, rows_b_ready = sem("rows_a_ready"), sem("rows_b_ready")
        tables_a_out, table_b_out = sem("tables_a_out"), sem("table_b_out")
        mod_ready = sem("mod_ready")
        w1_hi_ready, w1_lo_ready = sem("w1_hi_ready"), sem("w1_lo_ready")
        w2_hi_ready, w2_lo_ready = sem("w2_hi_ready"), sem("w2_lo_ready")
        gated = sem("gated")

        class Pipe:

            def __init__(self, tag):
                self.stats_done = sem(f"{tag}_stats_done")
                self.mean_done = sem(f"{tag}_mean_done")
                self.var_ready = sem(f"{tag}_var_ready")
                self.rstd_ready = sem(f"{tag}_rstd_ready")
                self.xhat_ready = sem(f"{tag}_xhat_ready")
                self.x_turned = sem(f"{tag}_x_turned")
                self.y_hi_ready = sem(f"{tag}_y_hi_ready")
                self.y_lo_ready = sem(f"{tag}_y_lo_ready")
                self.h_summed = sem(f"{tag}_h_summed")
                self.h_hi_ready = sem(f"{tag}_h_hi_ready")
                self.h_lo_ready = sem(f"{tag}_h_lo_ready")
                self.o_summed = sem(f"{tag}_o_summed")
                self.out_ready = sem(f"{tag}_out_ready")

        a, b = Pipe("a"), Pipe("b")
        a_idx_ln, a_idx_out = sem("a_idx_ln"), sem("a_idx_out")
        a_x_in, a_tab_in = sem("a_x_in"), sem("a_tab_in")
        a_res_in = sem("a_res_in")
        a_scaled, a_biased = sem("a_scaled"), sem("a_biased")
        a_stored, a_filled = sem("a_stored"), sem("a_filled")
        b_x_in = [sem("b_x_in0"), sem("b_x_in1")]
        b_gate_in = [sem("b_gate_in0"), sem("b_gate_in1")]
        b_idx_over, b_over_in = sem("b_idx_over"), sem("b_over_in")
        b_mod_cur, b_based = sem("b_mod_cur"), sem("b_based")
        waited = sem("waited")
        b_stored = [sem("b_stored0"), sem("b_stored1")]

        block = ctx.enter_context(nc.Block())

        def thirds(w):
            return w.rearrange("(k p) (c n) -> c p k n", p=P, c=3)

        def wait_alone(eng, semaphore, value):
            eng.wait_ge(semaphore, value)
            eng.sem_inc(waited, 1)

        def runs_of(eng):
            eng.wait_ge(runs_ready, 1)
            return eng.value_load(runs[0:1, 0:1], min_val=1, max_val=C // J - 1)

        @block.sync
        def _(sp):
            with nc.allow_non_contiguous_dma(reason="four mask bytes, single biases"):
                sp.dma_start(mask_u8[:, :].rearrange("p (b j) -> p b j", j=J),
                             mask.rearrange("b (p j) -> p b j", j=J)).then_inc(mask_in, DMA)
            for u in range(2):
                sp.sem_inc(b_stored[u], FREE)
            sp.dma_start(cond_sb, cond).then_inc(cond_in, DMA)
            for c in range(3):
                sp.dma_start(stage[:, c, :, :], thirds(ada_w)[c]).then_inc(ada_in[c], DMA)
            def to_rows(vec):
                return vec.rearrange("(o w d) -> o w d", o=1, d=D).to_broadcast([B, vec.shape[0] // D, D])

            sp.dma_start(rows_a[:, 0:1, :], to_rows(ada_b[D:2 * D])).then_inc(bias_in, DMA)
            sp.dma_start(rows_a[:, 1:2, :], to_rows(ada_b[0:D])).then_inc(bias_in, DMA)
            sp.dma_start(rows_a[:, 2:3, :], to_rows(ada_b[2 * D:3 * D])).then_inc(bias_in, DMA)
            sp.dma_start(rows_a[:, 3:4, :], to_rows(ssm_b2)).then_inc(bias_in, DMA)
            sp.dma_start(b2_bwd.rearrange("p (o d) -> p o d", o=1), to_rows(bwd_b2)).then_inc(bias_in, DMA)
            sp.dma_start(rows_b[:, 0:1, :], to_rows(ffada_b[2 * D:3 * D])).then_inc(bias_in, DMA)
            sp.dma_start(rows_b[:, 1:2, :], to_rows(ff_b2)).then_inc(bias_in, DMA)
            raw = raw_w1.rearrange("p (k t) d -> p k t d", k=K)
            sp.dma_start(raw[:, :, 0, :], ssm_w1.rearrange("(k p) n -> p k n", p=P)).then_inc(raw_w1_in, DMA)
            sp.dma_start(raw[:, :, 1, :], bwd_w1.rearrange("(k p) n -> p k n", p=P)).then_inc(raw_w1_in, DMA)
            with nc.allow_non_contiguous_dma(reason="single biases"):
                sp.dma_start(b1_a[:, 0:HALF], ssm_b1.rearrange("(m p) -> p m", p=P)).then_inc(b1_in, DMA)
                sp.dma_start(b1_a[:, HALF:M], bwd_b1.rearrange("(m p) -> p m", p=P)).then_inc(b1_in, DMA)
                sp.dma_start(b1_b[:, :], ff_b1.rearrange("(m p) -> p m", p=P)).then_inc(b1_in, DMA)
                sp.dma_start(mod_bias[:, :, :], ffada_b[0:2 * D].rearrange("(t k p) -> p t k", p=P, k=K)
                             ).then_inc(b1_in, DMA)
            for c in range(3):
                sp.wait_ge(ada_done, c + 1)
                sp.dma_start(stage[:, c, :, :], thirds(ffada_w)[c]).then_inc(ada_in[3 + c], DMA)
            sp.wait_ge(rows_a_ready, 1)
            sp.dma_start(table_ln.rearrange("b (t d) -> b t d", t=2), rows_a[:, 0:2, :]).then_inc(tables_a_out, DMA)
            sp.dma_start(table_out.rearrange("b (t d) -> b t d", t=2), rows_a[:, 2:4, :]).then_inc(tables_a_out, DMA)
            for c, w2 in enumerate((ssm_w2, bwd_w2)):
                sp.wait_ge(ada_done, 4 + c)
                sp.dma_start(stage[:, c, :, :], w2.rearrange("(m p) n -> p m n", p=P)).then_inc(raw_w2_in, DMA)
            sp.wait_ge(rows_b_ready, 1)
            sp.dma_start(table_b.rearrange("b (t d) -> b t d", t=2), rows_b).then_inc(table_b_out, DMA)
            sp.wait_ge(w2_hi_ready, 1)
            sp.wait_ge(w2_lo_ready, 1)
            sp.dma_start(stage_raw.rearrange("p (k n) -> p k n", k=K),
                         ff_w1.rearrange("(k p) n -> p k n", p=P)).then_inc(ff_w1_in, DMA)

            end = runs_of(sp)
            fill_end = sp.value_load(runs[0:1, 1:2], min_val=FEW + 1, max_val=C // J + 1)
            with sp.Fori(end + 1, fill_end) as i:
                sp.dma_start(compact_blocks[bass.ds(i, 1)].rearrange("o p j d -> (o p) j d"), stage[:, 2, :, :]
                             ).then_inc(a_filled, DMA)

            def load_row(s, u):
                sp.dma_start(x_sb[u], x_tiles[bass.ds(s, 1)].rearrange("o p j d -> (o p) j d")
                             ).then_inc(b_x_in[u], DMA)
                sp.dma_start(gate_sb[u], table_b[bass.ds(s, 1), :].rearrange("o (t d) -> o t d", t=2)
                             .to_broadcast([P, 2, D])).then_inc(b_gate_in[u], DMA)

            sp.wait_ge(table_b_out, DMA)
            sp.wait_ge(a_x_in, J * DMA * end + 2 * J * DMA)
            sp.wait_ge(a_tab_in, J * DMA * end + 2 * J * DMA)
            sp.wait_ge(a.xhat_ready, J * end + J)
            load_row(0, 0)
            load_row(1, 1)
            for c in range(2):
                sp.wait_ge(w1_hi_ready, K + (c + 1) * K // 2)
                sp.wait_ge(w1_lo_ready, K + (c + 1) * K // 2)
                sp.dma_start(stage[:, c, :, :], ff_w2.rearrange("(c m p) n -> c p m n", c=2, p=P)[c]
                             ).then_inc(ff_w2_in, DMA)
            with sp.Fori(0, B // 2) as i:
                for u in range(2):
                    s = 2 * i + u
                    sp.wait_ge(b.out_ready, J * s + J)
                    sp.dma_start(out_tiles[bass.ds(s, 1)].rearrange("o p j d -> (o p) j d"), o_sb[u]
                                 ).then_inc(b_stored[u], DMA)
                    load_row((s + 2) % B, u)
            for u in range(2):
                sp.wait_ge(b_stored[u], DMA * (B // 2) + FREE)
                sp.wait_ge(b_x_in[u], DMA * (B // 2 + 1))
                sp.wait_ge(b_gate_in[u], DMA * (B // 2 + 1))

        @block.gpsimd
        def _(pool):
            def count_up(to, pattern, base, per_partition):
                nc.gpsimd.iota(to, pattern=pattern, base=base, channel_multiplier=per_partition,
                               allow_small_or_imprecise_dtypes=True).then_inc(consts_set, 1)

            count_up(diff, [[1, P]], 0, -1)
            nc.gpsimd.memset(ident, 0.0).then_inc(zeros_set, 1)
            count_up(col_no[:, :], [[0, 1]], 0, 1)
            count_up(slot_no[:, :], [[1, S]], 0, 0)
            count_up(slots[:, :], [[P, J]], 0, 1)
            nc.gpsimd.memset(minus_half[:, :], -0.5).then_inc(consts_set, 1)
            pool.wait_ge(zeros_set, 1)
            nc.gpsimd.affine_select(out=ident, in_=ident, compare_op=ALU.not_equal, fill=1.0, base=0,
                                    pattern=[[-1, P]], channel_multiplier=1).then_inc(ident_ready, 1)

            def power(pipe, t):
                pool.wait_ge(pipe.var_ready, t + 1)
                nc.gpsimd.tensor_tensor(out=rstd[:, :], in0=var_eps[:, :], in1=minus_half[:, :],
                                        op=ALU.pow).then_inc(pipe.rstd_ready, 1)

            def gather(to, table, index, done):
                nc.gpsimd.indirect_dma_start(out=to, out_offset=None, in_=table,
                                             in_offset=bass.IndirectOffsetOnAxis(ap=index, axis=0)).then_inc(done, DMA)

            def gather_x(t):
                wait_alone(pool, a_idx_ln, t + 1)
                for j in range(J):
                    gather(xg[:, j, :], x_rows, idx_ln[:, 0, j:j + 1], a_x_in)

            def gather_modulation():
                for j in range(J):
                    gather(tab_ln[:, j, :], table_ln, idx_ln[:, 1, j:j + 1], a_tab_in)

            def gather_residual(i):
                wait_alone(pool, a_idx_out, i + 1)
                for j in range(J):
                    gather(tab_out[:, j, :], table_out, idx_out[:, 1, j:j + 1], a_res_in)
                for j in range(J):
                    gather(xr[:, j, :], x_rows, idx_out[:, 0, j:j + 1], a_res_in)

            def store_new(i):
                wait_alone(pool, a.out_ready, J * i + J)
                pool.dma_start(compact_blocks[bass.ds(i, 1)].rearrange("o p j d -> (o p) j d"), xr
                               ).then_inc(a_stored, DMA)
                wait_alone(pool, a_stored, DMA * i + DMA)

            gather_x(0)
            power(a, 0)
            pool.wait_ge(tables_a_out, 2 * DMA)
            gather_modulation()
            gather_x(1)
            gather_modulation()
            pool.wait_ge(w1_hi_ready, K)
            pool.wait_ge(w1_lo_ready, K)
            pool.wait_ge(table_b_out, DMA)
            end = runs_of(pool)
            with pool.Fori(0, end) as i:
                gather_residual(i)
                power(a, i + 1)
                gather_x(i + 2)
                gather_modulation()
                store_new(i)

            def overlay(u, loads, blocks):
                wait_alone(pool, b_x_in[u], DMA * loads)
                for j in range(J):
                    nc.gpsimd.indirect_dma_start(
                        out=x_sb[u][:, j, :], out_offset=None, in_=compact[0:blocks * S, :],
                        in_offset=bass.IndirectOffsetOnAxis(ap=idx_over[:, j:j + 1], axis=0),
                        bounds_check=blocks * S - 1, oob_is_err=False).then_inc(b_over_in, DMA)

            wait_alone(pool, b_idx_over, 1)
            overlay(0, 1, 1)
            power(b, 0)
            gather_residual(end)
            store_new(end)
            fills = pool.value_load(runs[0:1, 2:3], min_val=1, max_val=C // J)
            wait_alone(pool, a_filled, DMA * fills)

            def overlay_rest(blocks):
                with pool.Fori(0, B // 2) as i:
                    for u in range(2):
                        s = 2 * i + u
                        wait_alone(pool, b_idx_over, s + 2)
                        overlay(1 - u, i + 1 + u, blocks)
                        power(b, s + 1)

            with pool.If(end <= FEW - 1):
                overlay_rest(FEW)
            with pool.Else():
                overlay_rest(C // J)

        @block.scalar
        def _(act):
            act.wait_ge(cond_in, DMA)
            nc.scalar.activation(silu_sb, cond_sb, ACT.Silu).then_inc(silu_done, 1)

            def cut_w1(raw):
                for k in range(K):
                    nc.scalar.activation(w1_hi[:, k, :], raw[:, k * HID:(k + 1) * HID], ACT.Copy
                                         ).then_inc(w1_hi_ready, 1)

            def cut_w2():
                nc.scalar.activation(w2_hi[:, :, :].rearrange("p k n -> p (k n)"), stage_raw, ACT.Copy
                                     ).then_inc(w2_hi_ready, 1)

            act.wait_ge(raw_w1_in, 2 * DMA)
            cut_w1(raw_w1.rearrange("p t d -> p (t d)"))

            def cut_hidden(pipe, s, b1, func):
                for m in range(M):
                    act.wait_ge(pipe.h_summed, M * s + m + 1)
                    if m >= 2:
                        act.wait_ge(pipe.h_lo_ready, M * s + m - 1)
                    nc.scalar.activation(full[:, m % 2, :], ps_h[m % 2][:, :], func, bias=b1[:, m:m + 1])
                    nc.scalar.activation(h_hi[:, m, :], ps_h[m % 2][:, :], func,
                                         bias=b1[:, m:m + 1]).then_inc(pipe.h_hi_ready, 1)

            def cut_input(pipe, t, u):
                for k in range(K):
                    act.wait_ge(pipe.x_turned, K * t + k + 1)
                    if k >= 2:
                        act.wait_ge(pipe.y_lo_ready, K * t + k - 1)
                    for to in (full[:, 2 + k % 2, :], y_hi[:, k, :]):
                        if u is None:
                            last = nc.scalar.activation(to, ps_x[k % 2][:, :], ACT.Copy)
                        else:
                            last = nc.scalar.activation(to, ps_x[k % 2][:, :], ACT.Identity,
                                                        scale=mod_cur[:, u, 0, k:k + 1], bias=mod_cur[:, u, 1, k:k + 1])
                    last.then_inc(pipe.y_hi_ready, 1)

            cut_input(a, 0, None)
            act.wait_ge(raw_w2_in, 2 * DMA)
            cut_w2()
            act.wait_ge(b1_in, 4 * DMA)
            end = runs_of(act)
            with act.Fori(0, end) as i:
                cut_hidden(a, i, b1_a, ACT.Gelu)
                cut_input(a, i + 1, None)

            cut_hidden(a, end, b1_a, ACT.Gelu)
            act.wait_ge(ff_w1_in, DMA)
            cut_w1(stage_raw)
            act.wait_ge(b_mod_cur, 1)
            cut_input(b, 0, 0)
            act.wait_ge(a.o_summed, end + 1)
            act.wait_ge(ff_w2_in, 2 * DMA)
            cut_w2()
            with act.Fori(0, B // 2) as i:
                for u in range(2):
                    s = 2 * i + u
                    cut_hidden(b, s, b1_b, ACT.Gelu_apprx_tanh)
                    act.wait_ge(b_mod_cur, s + 2)
                    cut_input(b, s + 1, 1 - u)

        @block.vector
        def _(dve):
            steps = [0]

            def link(ins):
                steps[0] += 1
                ins.then_inc(dve_step, 1)
                dve.wait_ge(dve_step, steps[0])

            dve.sem_inc(gated, FREE)

            nc.vector.memset(ones[:, :], 1.0)
            dve.wait_ge(mask_in, DMA)
            nc.vector.tensor_copy(mask_bf[:, :], mask_u8[:, :]).then_inc(mask_ready, 1)
            dve.wait_ge(consts_set, 5)
            nc.vector.tensor_scalar(upto[:, :], diff, 0.0, None, ALU.is_ge).then_inc(mask_ready, 1)
            nc.vector.tensor_scalar(before, diff, 0.0, None, ALU.is_gt).then_inc(mask_ready, 1)
            dve.wait_ge(totals_ps, 1)
            link(nc.vector.tensor_copy(total[:, :], ps_x[1][:, 0:1]))
            nc.vector.tensor_scalar(totals[:, :], ones[:, :], total[:, 0:1], None, ALU.mult).then_inc(totals_ready, 1)
            nc.vector.tensor_scalar(totals_before, before, total[:, 0:1], None,
                                    ALU.mult).then_inc(totals_ready, 1)
            bits_j, bits_s = J.bit_length() - 1, S.bit_length() - 1
            link(nc.vector.tensor_copy(col_bits[:, 0:1], col_no[:, :]))
            nc.vector.tensor_scalar(col_bits[:, 1:2], col_bits[:, 0:1], bits_j, bits_s, ALU.logical_shift_right,
                                    ALU.logical_shift_left)
            link(nc.vector.tensor_scalar(col_bits[:, 2:3], col_bits[:, 0:1], J - 1, None, ALU.bitwise_and))
            link(nc.vector.tensor_tensor(col_bits[:, 0:1], col_bits[:, 1:2], col_bits[:, 2:3], ALU.bitwise_or))
            dve.wait_ge(ranks_ps, 1)
            nc.vector.tensor_copy(finder[:, 0:P - 1], ps_h[0][:, 0:P - 1])
            link(nc.vector.tensor_copy(edges[:, 1:2], ps_h[0][:, P - 1:P]))
            link(nc.vector.tensor_tensor(edges[:, 0:1], edges[:, 1:2], total[:, :], ALU.subtract))
            link(nc.vector.tensor_copy(finder[:, P - 1:P], col_bits[:, 0:1]))

            def own(ins, steps, count):
                ins.then_inc(steps, 1)
                wait_alone(dve, steps, count)

            def choose_columns(t, column_of, scratch):
                own(nc.vector.tensor_scalar(scratch, slot_no[:, :], edges[:, 1:2], None, ALU.is_lt),
                    slot_cols, 3 * t + 1)
                own(nc.vector.scalar_tensor_tensor(out=column_of, in0=slot_no[:, :], scalar=edges[:, 0:1],
                                                   in1=scratch, op0=ALU.is_ge, op1=ALU.mult), slot_cols, 3 * t + 2)
                own(nc.vector.tensor_scalar(edges[:, :], edges[:, :], -float(S), None, ALU.add),
                    slot_cols, 3 * t + 3)

            def find_tokens(t, ps, scratch):
                found = ps.rearrange("p (j i) -> p j i", j=J)
                upto_slot = scratch.rearrange("p (j i) -> p j i", j=J)[:, :, 0:P - 1]
                wait_alone(dve, places_ps, t + 1)
                own(nc.vector.tensor_tensor(upto_slot, found[:, :, 0:P - 1],
                                               slots[:, :].rearrange("p (j o) -> p j o", o=1)
                                               .to_broadcast([P, J, P - 1]), ALU.is_le), places_read, 4 * t + 1)
                own(nc.vector.tensor_reduce(place[:, :], upto_slot, AX.X, ALU.add), places_read, 4 * t + 2)
                tok = tok_no[:, bass.ds(J * t, J)]
                own(nc.vector.scalar_tensor_tensor(out=tok, in0=place[:, :], scalar=float(J),
                                                      in1=found[:, :, P - 1], op0=ALU.mult, op1=ALU.add), places_read, 4 * t + 3)
                nc.vector.tensor_scalar(slots[:, :], slots[:, :], float(S), None, ALU.add)
                own(nc.vector.tensor_scalar(row_no[:, bass.ds(J * t, J)], tok, bits_s, None,
                                               ALU.logical_shift_right), places_read, 4 * t + 4)

            def copy_numbers(to, t):
                nc.vector.tensor_copy(to[:, 0, :], tok_no[:, bass.ds(J * t, J)])
                return nc.vector.tensor_copy(to[:, 1, :], row_no[:, bass.ds(J * t, J)])

            choose_columns(0, xhat[:, 0, :], xhat[:, 1, :])
            choose_columns(1, xhat[:, 2, :], xhat[:, 3, :])
            dve.wait_ge(cond_turned, 1)
            nc.vector.tensor_copy(siluT, ps_o[3][:, 0:K * B].rearrange("p (k b) -> p k b", k=K)).then_inc(siluT_ready, 1)
            find_tokens(0, ps_x[0][:, :], xhat[:, 1, :])
            copy_numbers(idx_ln, 0).then_inc(a_idx_ln, 1)
            find_tokens(1, ps_x[1][:, :], xhat[:, 3, :])

            link(nc.vector.tensor_copy(runs_f[0:1, 0:1], ps_h[0][0:1, P:P + 1]))
            link(nc.vector.tensor_scalar(runs_f[0:1, 1:2], runs_f[0:1, 0:1], float(S + 1), float(S - 1),
                                         ALU.max, ALU.add))
            link(nc.vector.tensor_scalar(runs_f[0:1, 2:3], runs_f[0:1, 1:2], 1.0 / S, -(S - 1) / (2.0 * S) - 1.0,
                                         ALU.mult, ALU.add))
            link(nc.vector.tensor_copy(runs[0:1, 0:1], runs_f[0:1, 2:3]))
            link(nc.vector.tensor_copy(runs_f[0:1, 3:4], runs[0:1, 0:1]))
            link(nc.vector.tensor_scalar(runs_f[0:1, 4:5], runs_f[0:1, 3:4], float(FEW - 1), float(C // J - FEW),
                                         ALU.is_gt, ALU.mult))
            link(nc.vector.tensor_scalar(runs[0:1, 1:2], runs_f[0:1, 4:5], float(FEW + 1), None, ALU.add))
            link(nc.vector.tensor_scalar(runs_f[0:1, 5:6], runs_f[0:1, 3:4], -float(S), None, ALU.mult))
            link(nc.vector.tensor_tensor(runs_f[0:1, 5:6], runs_f[0:1, 5:6], runs_f[0:1, 0:1], ALU.add))
            link(nc.vector.tensor_scalar(runs[0:1, 3:4], runs_f[0:1, 5:6], 1.0, None, ALU.max))
            link(nc.vector.tensor_scalar(runs_f[0:1, 3:4], runs_f[0:1, 3:4], 1.0, None, ALU.add))
            nc.vector.tensor_tensor(runs[0:1, 2:3], runs[0:1, 1:2], runs_f[0:1, 3:4],
                                    ALU.subtract).then_inc(runs_ready, 1)

            link(nc.vector.tensor_scalar(is_none, mask_bf[:, :], -(NONE + 1.0), NONE, ALU.mult, ALU.add))
            link(nc.vector.tensor_tensor(over_no[:, 0:C], ps_h[1][:, 0:C], is_none, ALU.add))
            link(nc.vector.memset(over_no[:, C:C + J], int(NONE)))

            def statistics(pipe, t, tokens):
                for j in range(J):
                    nc.vector.bn_stats(stats[:, j, :], tokens[:, j, :]).then_inc(pipe.stats_done, 1)
                wait_alone(dve, pipe.stats_done, J * t + J)
                for j in range(J):
                    nc.vector.bn_aggr(mean_var[:, j, :], stats[:, j, :]).then_inc(pipe.mean_done, 1)
                dve.wait_ge(pipe.mean_done, J * t + J)
                nc.vector.tensor_scalar(var_eps[:, :], mean_var[:, :, 1], EPS, None, ALU.add).then_inc(pipe.var_ready, 1)

            def normal(j, tokens):
                return nc.vector.tensor_scalar(xhat[:, j, :], tokens[:, j, :], mean_var[:, j, 0:1], rstd[:, j:j + 1],
                                               ALU.subtract, ALU.mult)

            def low_input(pipe, t):
                for k in range(K):
                    dve.wait_ge(pipe.y_hi_ready, K * t + k + 1)
                    nc.vector.tensor_tensor(y_lo[:, k, :], full[:, 2 + k % 2, :], y_hi[:, k, :].bitcast(F32),
                                            ALU.subtract).then_inc(pipe.y_lo_ready, 1)

            def low_hidden(pipe, s, between):
                for m in range(M):
                    dve.wait_ge(pipe.h_hi_ready, M * s + m + 1)
                    nc.vector.tensor_tensor(h_lo[:, m, :], full[:, m % 2, :], h_hi[:, m, :].bitcast(F32),
                                            ALU.subtract).then_inc(pipe.h_lo_ready, 1)
                    between(m)

            def low_w1(raw, chunks):
                for k in range(K):
                    dve.wait_ge(w1_hi_ready, chunks + k + 1)
                    nc.vector.tensor_tensor(w1_lo[:, k, :], raw[:, k * HID:(k + 1) * HID],
                                            w1_hi[:, k, :].bitcast(F32), ALU.subtract).then_inc(w1_lo_ready, 1)

            def low_w2(times):
                dve.wait_ge(w2_hi_ready, times)
                nc.vector.tensor_tensor(w2_lo[:, :, :].rearrange("p k n -> p (k n)"), stage_raw,
                                        w2_hi[:, :, :].rearrange("p k n -> p (k n)").bitcast(F32),
                                        ALU.subtract).then_inc(w2_lo_ready, 1)

            def modulate_a(t):
                dve.wait_ge(a_tab_in, J * DMA * t + J * DMA)
                for j in range(J):
                    dve.wait_ge(a_scaled, 2 * J * t + j + 1)
                    nc.vector.tensor_tensor(xhat[:, j, :], xhat[:, j, :], tab_ln[:, j, 0:D],
                                            ALU.mult).then_inc(a_scaled, 1)
                for j in range(J):
                    dve.wait_ge(a_scaled, 2 * J * t + J + j + 1)
                    nc.vector.tensor_tensor(xhat[:, j, :], xhat[:, j, :], tab_ln[:, j, D:2 * D],
                                            ALU.add).then_inc(a.xhat_ready, 1)

            def statistics_a(t):
                dve.wait_ge(a_x_in, J * DMA * t + J * DMA)
                statistics(a, t, xg)

            def normal_a(t):
                dve.wait_ge(a.rstd_ready, t + 1)
                for j in range(J):
                    normal(j, xg).then_inc(a_scaled, 1)

            statistics_a(0)

            dve.wait_ge(bias_in, 7 * DMA)
            link(nc.vector.tensor_tensor(rows_a[:, 3, :], rows_a[:, 3, :], b2_bwd, ALU.add))
            for c, to in enumerate((1, 0, 2)):
                dve.wait_ge(ada_done, c + 1)
                link(nc.vector.tensor_tensor(rows_a[:, to, :], ps_o[c][0:B, :], rows_a[:, to, :], ALU.add))
            nc.vector.tensor_scalar(rows_a[:, 0, :], rows_a[:, 0, :], 1.0, None, ALU.add)
            nc.vector.tensor_tensor(rows_a[:, 3, :], rows_a[:, 2, :], rows_a[:, 3, :], ALU.mult
                                    ).then_inc(rows_a_ready, 1)

            normal_a(0)
            low_w1(raw_w1.rearrange("p t d -> p (t d)"), 0)
            modulate_a(0)
            copy_numbers(idx_ln, 1).then_inc(a_idx_ln, 1)

            dve.wait_ge(b1_in, 4 * DMA)
            link(nc.vector.memset(mod_b[:, B, :, :], 0.0))
            link(nc.vector.tensor_scalar(mod_bias[:, 1, :], mod_bias[:, 1, :], 1.0, None, ALU.add))
            dve.wait_ge(ada_done, 5)
            for c, to in enumerate((1, 0)):
                last = nc.vector.tensor_tensor(
                    mod_b[:, 0:B, to, :],
                    ps_h[0][:, c * K * B:(c + 1) * K * B].rearrange("p (k b) -> p b k", k=K),
                    mod_bias[:, c:c + 1, :].to_broadcast([P, B, K]), ALU.add)
            last.then_inc(mod_ready, 1)
            dve.wait_ge(ada_done, 6)
            link(nc.vector.tensor_tensor(rows_b[:, 0, :], ps_o[2][0:B, :], rows_b[:, 0, :], ALU.add))
            nc.vector.tensor_tensor(rows_b[:, 1, :], rows_b[:, 0, :], rows_b[:, 1, :], ALU.mult
                                    ).then_inc(rows_b_ready, 1)

            low_input(a, 0)
            low_w2(1)
            wait_alone(dve, a.y_lo_ready, K)
            choose_columns(2, full[:, 2, :], full[:, 3, :])

            def new_rows(i):
                dve.wait_ge(a_res_in, 2 * J * DMA * i + 2 * J * DMA)
                for j in range(J):
                    nc.vector.tensor_tensor(xr[:, j, :], xr[:, j, :], tab_out[:, j, D:2 * D],
                                            ALU.add).then_inc(a_biased, 1)
                dve.wait_ge(a.o_summed, i + 1)
                for j in range(J):
                    nc.vector.tensor_tensor(tab_out[:, j, 0:D], ps_o[j][:, :], tab_out[:, j, 0:D],
                                            ALU.mult).then_inc(gated, 1)
                for j in range(J):
                    dve.wait_ge(gated, J * i + j + 1 + FREE)
                    dve.wait_ge(a_biased, J * i + j + 1)
                    nc.vector.tensor_tensor(xr[:, j, :], xr[:, j, :], tab_out[:, j, 0:D],
                                            ALU.add).then_inc(a.out_ready, 1)

            end = runs_of(dve)
            with dve.Fori(0, end) as i:
                copy_numbers(idx_out, i).then_inc(a_idx_out, 1)

                def between(m):
                    if m == 1:
                        find_tokens(i + 2, ps_x[0][:, :], full[:, 3, :])
                    if m == 2:
                        statistics_a(i + 1)
                    if m == 4:
                        normal_a(i + 1)

                low_hidden(a, i, between)
                modulate_a(i + 1)
                copy_numbers(idx_ln, i + 2).then_inc(a_idx_ln, 1)
                low_input(a, i + 1)
                wait_alone(dve, a.y_lo_ready, K * i + 2 * K)
                choose_columns(i + 3, full[:, 2, :], full[:, 3, :])
                new_rows(i)

            def copy_current(t, u):
                nc.vector.tensor_copy(idx_over[:, :], over_no[:, bass.ds(J * t, J)]).then_inc(b_idx_over, 1)
                nc.vector.tensor_copy(mod_cur[:, u, :, :], mod_b[:, bass.ds(t, 1), :, :].rearrange(
                    "p o t k -> p (o t) k")).then_inc(b_mod_cur, 1)

            def statistics_b(t, u, in_count):
                dve.wait_ge(b_over_in, J * DMA * t + J * DMA)
                dve.wait_ge(b_gate_in[u], in_count)
                statistics(b, t, x_sb[u])

            def normal_b(t, u):
                dve.wait_ge(b.rstd_ready, t + 1)
                for j in range(J):
                    normal(j, x_sb[u]).then_inc(b.xhat_ready, 1)

            def add_bias(u):
                for j in range(J):
                    nc.vector.tensor_tensor(x_sb[u][:, j, :], x_sb[u][:, j, :], gate_sb[u][:, 1, :],
                                            ALU.add).then_inc(b_based, 1)

            copy_numbers(idx_out, end).then_inc(a_idx_out, 1)
            copy_current(0, 0)

            def between(m):
                if m == 3:
                    statistics_b(0, 0, DMA)
                if m == 4:
                    normal_b(0, 0)

            low_hidden(a, end, between)
            low_w1(stage_raw, K)
            low_input(b, 0)
            new_rows(end)
            add_bias(0)
            low_w2(2)
            with dve.Fori(0, B // 2) as i:
                for u in range(2):
                    s = 2 * i + u
                    copy_current(s + 1, 1 - u)

                    def between(m):
                        if m == 3:
                            statistics_b(s + 1, 1 - u, DMA * (i + 1) + DMA * u)
                        if m == 5:
                            normal_b(s + 1, 1 - u)

                    low_hidden(b, s, between)
                    add_bias(1 - u)
                    low_input(b, s + 1)
                    dve.wait_ge(b_stored[u], DMA * i + FREE)
                    dve.wait_ge(b.o_summed, s + 1)
                    for j in range(J):
                        nc.vector.tensor_tensor(o_sb[u][:, j, :], ps_o[j][:, :], gate_sb[u][:, 0, :],
                                                ALU.mult).then_inc(gated, 1)
                    for j in range(J):
                        dve.wait_ge(gated, J * s + J * end + J + j + 1 + FREE)
                        nc.vector.tensor_tensor(o_sb[u][:, j, :], o_sb[u][:, j, :], x_sb[u][:, j, :],
                                                ALU.add).then_inc(b.out_ready, 1)

        @block.tensor
        def _(pe):
            pe.wait_ge(mask_ready, 3)
            nc.tensor.matmul(ps_x[1][:, 0:1], mask_bf[:, :], ones[:, 0:1], start=True, stop=True).then_inc(totals_ps, 1)
            pe.wait_ge(ident_ready, 1)
            pe.wait_ge(silu_done, 1)
            for k in range(K):
                last = nc.tensor.transpose(ps_o[3][:, B * k:B * k + B], silu_sb[:, P * k:P * k + P], ident[0:B, 0:B])
            last.then_inc(cond_turned, 1)
            pe.wait_ge(totals_ready, 2)
            nc.tensor.matmul(ps_h[0][:, 0:P], mask_bf[:, :], upto[:, :], start=True, stop=False)
            nc.tensor.matmul(ps_h[0][:, 0:P], before, totals[:, :], start=False, stop=True)
            nc.tensor.matmul(ps_h[0][0:1, P:P + 1], totals[:, 0:1], ones[:, 0:1], start=True, stop=True)
            nc.tensor.matmul(ps_h[1][:, 0:C], upto[:, :], mask_bf[:, :], start=True, stop=False)
            nc.tensor.matmul(ps_h[1][:, 0:C], ones[:, :], totals_before, start=False, stop=True
                             ).then_inc(ranks_ps, 1)

            def look_up(t, ps, column_of):
                pe.wait_ge(slot_cols, 3 * t + 2)
                for j in range(J):
                    last = nc.tensor.matmul(ps[:, P * j:P * j + P], column_of[:, P * j:P * j + P], finder[:, :],
                                            start=True, stop=True)
                last.then_inc(places_ps, 1)

            look_up(0, ps_x[0], xhat[:, 0, :])
            look_up(1, ps_x[1], xhat[:, 2, :])

            pe.wait_ge(siluT_ready, 1)
            for c in range(3):
                pe.wait_ge(ada_in[c], DMA)
                for k in range(K):
                    last = nc.tensor.matmul(ps_o[c][0:B, :], siluT[:, k, :], stage[:, c, k, :],
                                            start=(k == 0), stop=(k == K - 1))
                last.then_inc(ada_done, 1)
            pe.wait_ge(rows_a_ready, 1)
            pe.wait_ge(runs_ready, 1)
            for c in range(2):
                pe.wait_ge(ada_in[3 + c], DMA)
                for f in range(K):
                    for k in range(K):
                        last = nc.tensor.matmul(ps_h[0][:, (c * K + f) * B:(c * K + f + 1) * B],
                                                stage[:, c, k, P * f:P * f + P], siluT[:, k, :],
                                                start=(k == 0), stop=(k == K - 1))
                last.then_inc(ada_done, 1)
            pe.wait_ge(ada_in[5], DMA)
            for k in range(K):
                last = nc.tensor.matmul(ps_o[2][0:B, :], siluT[:, k, :], stage[:, 2, k, :],
                                        start=(k == 0), stop=(k == K - 1))
            last.then_inc(ada_done, 1)

            def turn_chunk(pipe, t, k):
                if k == 0:
                    pe.wait_ge(pipe.xhat_ready, J * t + J)
                if k >= 2:
                    pe.wait_ge(pipe.y_hi_ready, K * t + k - 1)
                for j in range(J):
                    last = nc.tensor.transpose(ps_x[k % 2][:, P * j:P * j + P], xhat[:, j, P * k:P * k + P], ident)
                last.then_inc(pipe.x_turned, 1)

            def layer1(pipe, s, chunks, width, between):
                for m in range(M):
                    if m >= 2:
                        pe.wait_ge(pipe.h_hi_ready, M * s + m - 1)
                    for k in range(K):
                        if m == 0:
                            pe.wait_ge(pipe.y_hi_ready, K * s + k + 1)
                            pe.wait_ge(pipe.y_lo_ready, K * s + k + 1)
                            pe.wait_ge(w1_hi_ready, chunks + k + 1)
                            pe.wait_ge(w1_lo_ready, chunks + k + 1)
                        w_hi, w_lo = w1_hi[:, k, P * m:P * m + P], w1_lo[:, k, P * m:P * m + P]
                        to, hi, lo = ps_h[m % 2][:, 0:width], y_hi[:, k, 0:width], y_lo[:, k, 0:width]
                        nc.tensor.matmul(to, w_hi, hi, start=(k == 0), stop=False)
                        nc.tensor.matmul(to, w_hi, lo, start=False, stop=False)
                        last = nc.tensor.matmul(to, w_lo, hi, start=False, stop=(k == K - 1))
                    last.then_inc(pipe.h_summed, 1)
                    between(m)

            def layer2(pipe, s, free, weights, subs, turn):
                pe.wait_ge(w2_hi_ready, weights)
                pe.wait_ge(w2_lo_ready, weights)
                pe.wait_ge(gated, free)
                for m in range(M):
                    pe.wait_ge(pipe.h_hi_ready, M * s + m + 1)
                    pe.wait_ge(pipe.h_lo_ready, M * s + m + 1)
                    for j in range(subs):
                        hi, lo = h_hi[:, m, P * j:P * j + P], h_lo[:, m, P * j:P * j + P]
                        nc.tensor.matmul(ps_o[j][:, :], hi, w2_hi[:, m, :], start=(m == 0), stop=False)
                        nc.tensor.matmul(ps_o[j][:, :], hi, w2_lo[:, m, :], start=False, stop=False)
                        last = nc.tensor.matmul(ps_o[j][:, :], lo, w2_hi[:, m, :], start=False, stop=(m == M - 1))
                    if m == M - 1:
                        last.then_inc(pipe.o_summed, 1)
                    if m in TURN_AFTER:
                        turn(TURN_AFTER.index(m))

            for k in range(K):
                turn_chunk(a, 0, k)
            pe.wait_ge(mod_ready, 1)
            pe.wait_ge(rows_b_ready, 1)
            end = runs_of(pe)
            last_tokens = pe.value_load(runs[0:1, 3:4], min_val=1, max_val=S)
            with pe.Fori(0, end) as i:

                def between(m):
                    if m == 0:
                        look_up(i + 2, ps_x[0], full[:, 2, :])

                def turn(k):
                    if k == 0:
                        pe.wait_ge(places_read, 4 * i + 12)
                    turn_chunk(a, i + 1, k)

                layer1(a, i, 0, S, between)
                layer2(a, i, J * i + FREE, 1, J, turn)

            def last_supertile(width, subs):
                layer1(a, end, 0, width, lambda m: None)
                layer2(a, end, J * end + FREE, 1, subs, lambda k: turn_chunk(b, 0, k))

            with pe.If(last_tokens <= P):
                last_supertile(2 * P, 1)
            with pe.Else():
                last_supertile(S, J)

            with pe.Fori(0, B // 2) as i:
                for u in range(2):
                    s = 2 * i + u
                    layer1(b, s, K, S, lambda m: None)
                    layer2(b, s, J * s + J * end + J + FREE, 2, J, lambda k: turn_chunk(b, s + 1, k))


_INS = ['x', 'cond_1024', 'mask_BxS_bk0', 'L0_cond_ada_w', 'L0_cond_ada_b', 'L0_cond_ssm_w1', 'L0_cond_ssm_b1',
        'L0_cond_ssm_w2', 'L0_cond_ssm_b2', 'L0_cond_bwd_w1', 'L0_cond_bwd_b1', 'L0_cond_bwd_w2', 'L0_cond_bwd_b2',
        'L0_cond_ffada_w', 'L0_cond_ffada_b', 'L0_cond_ff_w1', 'L0_cond_ff_b1', 'L0_cond_ff_w2', 'L0_cond_ff_b2']


def kernel(**inputs):
    import numpy as _np
    import concourse.bacc as _bacc
    from concourse import mybir as _mybir
    from concourse.bass_utils import run_bass_kernel_spmd as _run

    nc = _bacc.Bacc("TRN2", target_bir_lowering=False, num_devices=1)
    arrays, args = {}, []
    for name in _INS:
        a = _np.ascontiguousarray(inputs[name])
        arrays[f"in_{name}"] = a
        args.append(nc.dram_tensor(f"in_{name}", a.shape, _mybir.dt.from_np(a.dtype), kind="ExternalInput").ap())
    shape = inputs['x'].shape
    args.append(nc.dram_tensor("out_0", shape, _mybir.dt.float32, kind="ExternalOutput").ap())
    build(nc, *args)
    r = _run(nc, [arrays], core_ids=[0])
    return r.results[0]["out_0"]
```

```python
from contextlib import ExitStack

import concourse.bass as bass
from concourse import mybir

F32 = mybir.dt.float32
BF16 = mybir.dt.bfloat16
F32R = mybir.dt.float32r
U32 = mybir.dt.uint32
I32 = mybir.dt.int32
U8 = mybir.dt.uint8
ALU = mybir.AluOpType
ACT = mybir.ActivationFunctionType
AX = mybir.AxisListType

P = 128
EPS = 1e-6
DMA = 16
FREE = 1


def build(nc, x, cond, mask, ada_w, ada_b, ssm_w1, ssm_b1, ssm_w2, ssm_b2, bwd_w1, bwd_b1, bwd_w2, bwd_b2,
          ffada_w, ffada_b, ff_w1, ff_b1, ff_w2, ff_b2, out):
    B, S, D = x.shape
    T = B * S
    K = D // P
    J = S // P
    HID = ff_w1.shape[1]
    M = HID // P
    C = T // P
    HALF = M // 2
    FEW = 8
    assert HID == 2 * D and S == D and J == K and J * B == P == C and T < 1 << 23 and FEW < C // J
    NONE = float(8 * T)
    TURN_AFTER = [2, 3, 4, 5]

    ctx = ExitStack()
    with ctx:
        def sb(name, shape, dt=F32):
            return ctx.enter_context(nc.sbuf_tensor(name, shape, dt))

        def sem(name):
            return ctx.enter_context(nc.semaphore(name))

        w1_hi = sb("w1_hi", [P, K, HID], F32R)
        w1_lo = sb("w1_lo", [P, K, HID], F32R)
        w2_hi = sb("w2_hi", [P, M, D], F32R)
        w2_lo = sb("w2_lo", [P, M, D], F32R)
        h_hi = sb("h_hi", [P, M, S], F32R)
        h_lo = sb("h_lo", [P, M, S], F32R)
        y_hi = sb("y_hi", [P, K, S], F32R)
        y_lo = sb("y_lo", [P, K, S], F32R)
        full = sb("full", [P, 4, S])
        xhat = sb("xhat", [P, J, D])
        stage = sb("stage", [P, 3, K, D])
        raw_w2 = [stage[:, 0, :, :], stage[:, 1, :, :]]
        raw_ff_w2 = [stage[:, 2, :, :], stage[:, 0, :, :]]
        stage_raw = stage[:, 0:2, :, :].rearrange("p c k d -> p (c k d)")
        region = sb("region", [P, 24, 512])
        xg = region[:, 0:4, :]
        tab_ln = region[:, 4:12, :].rearrange("p (j t) d -> p j (t d)", j=J)
        tab_out = region[:, 12:20, :].rearrange("p (j t) d -> p j (t d)", j=J)
        xr = region[:, 20:24, :]
        x_sb = [region[:, 0:4, :], region[:, 4:8, :]]
        gate_sb = [region[:, 8:10, :], region[:, 10:12, :]]
        o_sb = [region[:, 12:16, :], region[:, 16:20, :]]
        cond_sb = region[0:B, 4, :]
        silu_sb = region[0:B, 5, :]
        b2_bwd = region[0:B, 6, :]
        rows_ln = region[0:B, 8:10, :]
        rows_out = full[0:B, 2:4, :]
        raw_w1 = region[:, 12:20, :]
        rows_b = region[0:B, 20:22, :]
        shift_scale_b = full[0:B, 0:2, :]
        siluT = region[:, 22, 0:K * B].rearrange("p (k b) -> p k b", k=K)
        diff = region[:, 23, 0:P]
        halves = region[:, 23, P:3 * P].bitcast(BF16)
        before = halves[:, 0:P]
        totals_before = halves[:, P:2 * P]

        ident = sb("ident", [P, P])[:, :]
        upto = sb("upto", [P, P], BF16)
        ones = sb("ones", [P, P], BF16)
        mask_bf = sb("mask_bf", [P, C], BF16)
        totals = sb("totals", [P, P], BF16)
        total = sb("total", [P, 1])
        finder = sb("finder", [P, P])
        col_no = sb("col_no", [P, 1])
        col_bits = sb("col_bits", [P, 3], U32)
        edges = sb("edges", [P, 2])
        slot_no = sb("slot_no", [P, S])
        slots = sb("slots", [P, J])
        place = sb("place", [P, J])
        mod_b = sb("mod_b", [P, B, 2, K])
        mod_cur = sb("mod_cur", [P, 2, 2, K])
        b1_a = sb("b1_a", [P, M])
        b1_b = sb("b1_b", [P, M])
        mod_bias = sb("mod_bias", [P, 2, K])
        tok_no = sb("tok_no", [P, C + J], U32)
        row_no = sb("row_no", [P, C + J], U32)
        over_no = sb("over_no", [P, C], U32)
        idx_ln = sb("idx_ln", [P, 2, J], U32)
        idx_out = sb("idx_out", [P, 2, J], U32)
        idx_over = sb("idx_over", [P, J], U32)
        mask_u8 = sb("mask_u8", [P, C], U8)
        stats = sb("stats", [P, J, 6])
        mean_var = sb("mean_var", [P, J, 2])
        var_eps = sb("var_eps", [P, J])
        minus_half = sb("minus_half", [P, J])
        rstd = sb("rstd", [P, J])
        runs_f = sb("runs_f", [1, 6])
        last_slot = sb("last_slot", [1, 2], U32)
        runs = sb("runs", [1, 4], I32)
        is_none = full[:, 1, 0:C]

        ps_o = [ctx.enter_context(nc.psum_tensor(f"ps_o{j}", [P, 512], F32)) for j in range(J)]
        ps_h = [ctx.enter_context(nc.psum_tensor(f"ps_h{i}", [P, 512], F32)) for i in range(2)]
        ps_x = [ctx.enter_context(nc.psum_tensor(f"ps_x{i}", [P, 512], F32)) for i in range(2)]

        compact = nc.dram_tensor("compact_rows", [T + S, D], F32).ap()
        table_ln = nc.dram_tensor("table_ln", [B, 2 * D], F32).ap()
        table_out = nc.dram_tensor("table_out", [B, 2 * D], F32).ap()
        table_b = nc.dram_tensor("table_b", [B, 2 * D], F32).ap()
        x_rows = x.rearrange("b s d -> (b s) d")
        x_tiles = x.rearrange("b (p j) d -> b p j d", j=J)
        out_tiles = out.rearrange("b (p j) d -> b p j d", j=J)
        compact_blocks = compact.rearrange("(i j p) d -> i p j d", p=P, j=J)


        mask_in, cond_in, bias_in, b1_in = sem("mask_in"), sem("cond_in"), sem("bias_in"), sem("b1_in")
        ada_in = [sem(f"ada_in{i}") for i in range(6)]
        raw_w1_in, raw_w2_in = sem("raw_w1_in"), [sem("raw_w2_in0"), sem("raw_w2_in1")]
        ff_w1_in, ff_w2_in = sem("ff_w1_in"), [sem("ff_w2_in0"), sem("ff_w2_in1")]
        consts_set, zeros_set, ident_ready = sem("consts_set"), sem("zeros_set"), sem("ident_ready")
        silu_done, cond_turned, siluT_ready = sem("silu_done"), sem("cond_turned"), sem("siluT_ready")
        ada_done = sem("ada_done")
        dve_step = sem("dve_step")
        mask_ready, totals_ps, totals_ready, ranks_ps = (
            sem("mask_ready"), sem("totals_ps"), sem("totals_ready"), sem("ranks_ps"))
        slot_cols, places_ps, places_read = sem("slot_cols"), sem("places_ps"), sem("places_read")
        runs_ready = sem("runs_ready")
        rows_a_ready, rows_b_ready = sem("rows_a_ready"), sem("rows_b_ready")
        table_ln_out, table_out_out, table_b_out = sem("table_ln_out"), sem("table_out_out"), sem("table_b_out")
        mod_turned, mod_ready = sem("mod_turned"), sem("mod_ready")
        w1_hi_ready, w1_lo_ready = sem("w1_hi_ready"), sem("w1_lo_ready")
        w2_hi_ready, w2_lo_ready = sem("w2_hi_ready"), sem("w2_lo_ready")
        gated = sem("gated")

        class Pipe:

            def __init__(self, tag):
                self.stats_done = sem(f"{tag}_stats_done")
                self.mean_done = sem(f"{tag}_mean_done")
                self.var_ready = sem(f"{tag}_var_ready")
                self.rstd_ready = sem(f"{tag}_rstd_ready")
                self.xhat_ready = sem(f"{tag}_xhat_ready")
                self.x_turned = sem(f"{tag}_x_turned")
                self.y_hi_ready = sem(f"{tag}_y_hi_ready")
                self.y_lo_ready = sem(f"{tag}_y_lo_ready")
                self.h_summed = sem(f"{tag}_h_summed")
                self.h_hi_ready = sem(f"{tag}_h_hi_ready")
                self.h_lo_ready = sem(f"{tag}_h_lo_ready")
                self.o_summed = sem(f"{tag}_o_summed")
                self.out_ready = sem(f"{tag}_out_ready")

        a, b = Pipe("a"), Pipe("b")
        a_idx_ln, a_idx_out = sem("a_idx_ln"), sem("a_idx_out")
        a_x_in = sem("a_x_in")
        a_tab_in = [sem(f"a_tab_in{j}") for j in range(J)]
        a_res_in = sem("a_res_in")
        a_scaled, a_biased = sem("a_scaled"), sem("a_biased")
        a_stored, a_filled = sem("a_stored"), sem("a_filled")
        b_x_in = [sem("b_x_in0"), sem("b_x_in1")]
        b_gate_in = [sem("b_gate_in0"), sem("b_gate_in1")]
        b_idx_over, b_over_in = sem("b_idx_over"), sem("b_over_in")
        b_mod_cur, b_based = sem("b_mod_cur"), sem("b_based")
        waited = sem("waited")
        b_stored = [sem("b_stored0"), sem("b_stored1")]

        block = ctx.enter_context(nc.Block())

        def thirds(w):
            return w.rearrange("(k p) (c n) -> c p k n", p=P, c=3)

        def wait_alone(eng, semaphore, value):
            eng.wait_ge(semaphore, value)
            eng.sem_inc(waited, 1)

        def flat(ap):
            return ap.rearrange("p k n -> p (k n)")

        def halves_of(w2):
            return [flat(w2[:, K * c:K * c + K, :]) for c in range(2)]

        def runs_of(eng):
            eng.wait_ge(runs_ready, 1)
            return eng.value_load(runs[0:1, 0:1], min_val=2, max_val=C // J - 1)

        def tokens_of_last(eng):
            return eng.value_load(runs[0:1, 3:4], min_val=1, max_val=S)

        @block.sync
        def _(sp):
            with nc.allow_non_contiguous_dma(reason="four mask bytes, single biases"):
                sp.dma_start(mask_u8[:, :].rearrange("p (b j) -> p b j", j=J),
                             mask.rearrange("b (p j) -> p b j", j=J)).then_inc(mask_in, DMA)
            for u in range(2):
                sp.sem_inc(b_stored[u], FREE)
            sp.sem_inc(a_stored, DMA)
            sp.dma_start(cond_sb, cond).then_inc(cond_in, DMA)
            for c in range(3):
                sp.dma_start(stage[:, c, :, :], thirds(ada_w)[c]).then_inc(ada_in[c], DMA)
            def to_rows(vec):
                return vec.rearrange("(o w d) -> o w d", o=1, d=D).to_broadcast([B, vec.shape[0] // D, D])

            sp.dma_start(rows_ln[:, 0:1, :], to_rows(ada_b[D:2 * D])).then_inc(bias_in, DMA)
            sp.dma_start(rows_ln[:, 1:2, :], to_rows(ada_b[0:D])).then_inc(bias_in, DMA)
            sp.dma_start(rows_out[:, 0:1, :], to_rows(ada_b[2 * D:3 * D])).then_inc(bias_in, DMA)
            sp.dma_start(rows_out[:, 1:2, :], to_rows(ssm_b2)).then_inc(bias_in, DMA)
            sp.dma_start(b2_bwd.rearrange("p (o d) -> p o d", o=1), to_rows(bwd_b2)).then_inc(bias_in, DMA)
            sp.dma_start(rows_b[:, 0:1, :], to_rows(ffada_b[2 * D:3 * D])).then_inc(bias_in, DMA)
            sp.dma_start(rows_b[:, 1:2, :], to_rows(ff_b2)).then_inc(bias_in, DMA)
            raw = raw_w1.rearrange("p (k t) d -> p k t d", k=K)
            sp.dma_start(raw[:, :, 0, :], ssm_w1.rearrange("(k p) n -> p k n", p=P)).then_inc(raw_w1_in, DMA)
            sp.dma_start(raw[:, :, 1, :], bwd_w1.rearrange("(k p) n -> p k n", p=P)).then_inc(raw_w1_in, DMA)
            with nc.allow_non_contiguous_dma(reason="single biases"):
                sp.dma_start(b1_a[:, 0:HALF], ssm_b1.rearrange("(m p) -> p m", p=P)).then_inc(b1_in, DMA)
                sp.dma_start(b1_a[:, HALF:M], bwd_b1.rearrange("(m p) -> p m", p=P)).then_inc(b1_in, DMA)
                sp.dma_start(b1_b[:, :], ff_b1.rearrange("(m p) -> p m", p=P)).then_inc(b1_in, DMA)
                sp.dma_start(mod_bias[:, :, :], ffada_b[0:2 * D].rearrange("(t k p) -> p t k", p=P, k=K)
                             ).then_inc(b1_in, DMA)
            sp.wait_ge(rows_a_ready, 1)
            sp.dma_start(table_ln.rearrange("b (t d) -> b t d", t=2), rows_ln).then_inc(table_ln_out, DMA)
            for c in range(3):
                sp.wait_ge(ada_done, c + 1)
                sp.dma_start(stage[:, c, :, :], thirds(ffada_w)[c]).then_inc(ada_in[3 + c], DMA)
            sp.wait_ge(rows_a_ready, 2)
            sp.dma_start(table_out.rearrange("b (t d) -> b t d", t=2), rows_out).then_inc(table_out_out, DMA)
            for c, w2 in enumerate((ssm_w2, bwd_w2)):
                sp.wait_ge(ada_done, 4 + c)
                sp.dma_start(stage[:, c, :, :], w2.rearrange("(m p) n -> p m n", p=P)).then_inc(raw_w2_in[c], DMA)
            sp.wait_ge(rows_b_ready, 3)
            sp.dma_start(table_b.rearrange("b (t d) -> b t d", t=2), rows_b).then_inc(table_b_out, DMA)
            sp.wait_ge(w2_hi_ready, 2)
            sp.wait_ge(w2_lo_ready, 2)
            sp.dma_start(stage_raw.rearrange("p (k n) -> p k n", k=K),
                         ff_w1.rearrange("(k p) n -> p k n", p=P)).then_inc(ff_w1_in, DMA)

            def load_ff_w2(c):
                sp.dma_start(raw_ff_w2[c], ff_w2.rearrange("(c m p) n -> c p m n", c=2, p=P)[c]
                             ).then_inc(ff_w2_in[c], DMA)

            end = runs_of(sp)
            fill_end = sp.value_load(runs[0:1, 1:2], min_val=FEW + 1, max_val=C // J + 1)
            with sp.Fori(end + 1, fill_end) as i:
                sp.dma_start(compact_blocks[bass.ds(i, 1)].rearrange("o p j d -> (o p) j d"), stage[:, 2, :, :]
                             ).then_inc(a_filled, DMA)

            fills = sp.value_load(runs[0:1, 2:3], min_val=1, max_val=C // J)
            wait_alone(sp, a_filled, DMA * fills)
            load_ff_w2(0)

            def load_row(s, u):
                sp.dma_start(x_sb[u], x_tiles[bass.ds(s, 1)].rearrange("o p j d -> (o p) j d")
                             ).then_inc(b_x_in[u], DMA)
                sp.dma_start(gate_sb[u], table_b[bass.ds(s, 1), :].rearrange("o (t d) -> o t d", t=2)
                             .to_broadcast([P, 2, D])).then_inc(b_gate_in[u], DMA)

            def store_new(i):
                sp.wait_ge(a.out_ready, J * i + J)
                sp.dma_start(compact_blocks[bass.ds(i, 1)].rearrange("o p j d -> (o p) j d"), xr
                             ).then_inc(a_stored, DMA)

            with sp.Fori(0, end - 1) as i:
                store_new(i)
            sp.wait_ge(table_b_out, DMA)
            sp.wait_ge(a.xhat_ready, J * end + J)
            load_row(0, 0)
            store_new(end - 1)
            load_row(1, 1)
            sp.wait_ge(w1_hi_ready, K + K // 2)
            sp.wait_ge(w1_lo_ready, K + K // 2)
            load_ff_w2(1)
            store_new(end)
            def store_row(s, u):
                sp.wait_ge(b.out_ready, J * s + J)
                sp.dma_start(out_tiles[bass.ds(s, 1)].rearrange("o p j d -> (o p) j d"), o_sb[u]
                             ).then_inc(b_stored[u], DMA)

            with sp.Fori(0, B // 2 - 1) as i:
                for u in range(2):
                    store_row(2 * i + u, u)
                    load_row(2 * i + u + 2, u)
            store_row(B - 2, 0)
            for j in range(J):
                sp.wait_ge(b.out_ready, J * (B - 1) + j + 1)
                sp.dma_start(out_tiles[B - 1, :, j, :], o_sb[1][:, j, :]).then_inc(b_stored[1], DMA)
            sp.wait_ge(b_stored[0], DMA * (B // 2) + FREE)
            sp.wait_ge(b_stored[1], DMA * (B // 2 + J - 1) + FREE)

        @block.gpsimd
        def _(pool):
            def count_up(to, pattern, base, per_partition):
                nc.gpsimd.iota(to, pattern=pattern, base=base, channel_multiplier=per_partition,
                               allow_small_or_imprecise_dtypes=True).then_inc(consts_set, 1)

            count_up(diff, [[1, P]], 0, -1)
            nc.gpsimd.memset(ident, 0.0).then_inc(zeros_set, 1)
            count_up(col_no[:, :], [[0, 1]], 0, 1)
            count_up(slot_no[:, :], [[1, S]], 0, 0)
            count_up(slots[:, :], [[P, J]], 0, 1)
            nc.gpsimd.memset(minus_half[:, :], -0.5).then_inc(consts_set, 1)
            pool.wait_ge(zeros_set, 1)
            nc.gpsimd.affine_select(out=ident, in_=ident, compare_op=ALU.not_equal, fill=1.0, base=0,
                                    pattern=[[-1, P]], channel_multiplier=1).then_inc(ident_ready, 1)

            def power(pipe, t):
                pool.wait_ge(pipe.var_ready, t + 1)
                nc.gpsimd.tensor_tensor(out=rstd[:, :], in0=var_eps[:, :], in1=minus_half[:, :],
                                        op=ALU.pow).then_inc(pipe.rstd_ready, 1)

            def gather(to, table, index, done):
                nc.gpsimd.indirect_dma_start(out=to, out_offset=None, in_=table,
                                             in_offset=bass.IndirectOffsetOnAxis(ap=index, axis=0)).then_inc(done, DMA)

            def gather_x(t):
                wait_alone(pool, a_idx_ln, t + 1)
                for j in range(J):
                    gather(xg[:, j, :], x_rows, idx_ln[:, 0, j:j + 1], a_x_in)

            def gather_modulation():
                for j in range(J):
                    gather(tab_ln[:, j, :], table_ln, idx_ln[:, 1, j:j + 1], a_tab_in[j])

            def gather_residual(i):
                wait_alone(pool, a_idx_out, i + 1)
                for j in range(J):
                    gather(tab_out[:, j, :], table_out, idx_out[:, 1, j:j + 1], a_res_in)
                wait_alone(pool, a_stored, DMA * i + DMA)
                for j in range(J):
                    gather(xr[:, j, :], x_rows, idx_out[:, 0, j:j + 1], a_res_in)

            gather_x(0)
            pool.wait_ge(table_ln_out, DMA)
            gather_modulation()
            power(a, 0)
            gather_x(1)
            gather_modulation()

            def low_w2(raw, halves):
                for c in range(2):
                    pool.wait_ge(w2_hi_ready, halves + c + 1)
                    nc.gpsimd.tensor_tensor(halves_of(w2_lo)[c], flat(raw[c]), halves_of(w2_hi)[c].bitcast(F32),
                                            ALU.subtract).then_inc(w2_lo_ready, 1)

            low_w2(raw_w2, 0)
            pool.wait_ge(w1_hi_ready, K)
            pool.wait_ge(w1_lo_ready, K)
            pool.wait_ge(table_out_out, DMA)
            pool.wait_ge(table_b_out, DMA)
            end = runs_of(pool)
            with pool.Fori(0, end - 1) as i:
                power(a, i + 1)
                gather_residual(i)
                gather_x(i + 2)
                gather_modulation()
            power(a, end)
            gather_residual(end - 1)

            def overlay(u, loads, blocks):
                wait_alone(pool, b_x_in[u], DMA * loads)
                for j in range(J):
                    nc.gpsimd.indirect_dma_start(
                        out=x_sb[u][:, j, :], out_offset=None, in_=compact[0:blocks * S, :],
                        in_offset=bass.IndirectOffsetOnAxis(ap=idx_over[:, j:j + 1], axis=0),
                        bounds_check=blocks * S - 1, oob_is_err=False).then_inc(b_over_in, DMA)

            wait_alone(pool, b_idx_over, 1)
            pool.wait_ge(a_stored, 2 * DMA)
            overlay(0, 1, 1)
            power(b, 0)
            gather_residual(end)
            low_w2(raw_ff_w2, 2)
            wait_alone(pool, a_stored, DMA * end + 2 * DMA)
            fills = pool.value_load(runs[0:1, 2:3], min_val=1, max_val=C // J)
            wait_alone(pool, a_filled, DMA * fills)

            def overlay_rest(blocks):
                def prepare_next(s, u, loads):
                    wait_alone(pool, b_idx_over, s + 2)
                    overlay(1 - u, loads, blocks)
                    power(b, s + 1)

                with pool.Fori(0, B // 2 - 1) as i:
                    for u in range(2):
                        prepare_next(2 * i + u, u, i + 1 + u)
                prepare_next(B - 2, 0, B // 2)

            with pool.If(end <= FEW - 1):
                overlay_rest(FEW)
            with pool.Else():
                overlay_rest(C // J)

        @block.scalar
        def _(act):
            act.wait_ge(cond_in, DMA)
            nc.scalar.activation(silu_sb, cond_sb, ACT.Silu).then_inc(silu_done, 1)

            def cut_w1(raw, k):
                nc.scalar.activation(w1_hi[:, k, :], raw[:, k * HID:(k + 1) * HID], ACT.Copy).then_inc(w1_hi_ready, 1)

            def cut_w2(raw, raw_in, c):
                act.wait_ge(raw_in[c], DMA)
                nc.scalar.activation(halves_of(w2_hi)[c], flat(raw[c]), ACT.Copy).then_inc(w2_hi_ready, 1)

            act.wait_ge(raw_w1_in, 2 * DMA)
            for k in range(K):
                cut_w1(raw_w1.rearrange("p t d -> p (t d)"), k)

            def cut_hidden(pipe, s, b1, func, width=S):
                for m in range(M):
                    act.wait_ge(pipe.h_summed, M * s + m + 1)
                    if m >= 2:
                        act.wait_ge(pipe.h_lo_ready, M * s + m - 1)
                    whole, high, summed = full[:, m % 2, 0:width], h_hi[:, m, 0:width], ps_h[m % 2][:, 0:width]
                    nc.scalar.activation(whole, summed, func, bias=b1[:, m:m + 1])
                    nc.scalar.activation(high, summed, func,
                                         bias=b1[:, m:m + 1]).then_inc(pipe.h_hi_ready, 1)

            def cut_input(pipe, t, u, first=lambda k: None):
                for k in range(K):
                    first(k)
                    act.wait_ge(pipe.x_turned, K * t + k + 1)
                    if k >= 2:
                        act.wait_ge(pipe.y_lo_ready, K * t + k - 1)
                    for to in (full[:, 2 + k % 2, :], y_hi[:, k, :]):
                        if u is None:
                            last = nc.scalar.activation(to, ps_x[k % 2][:, :], ACT.Copy)
                        else:
                            last = nc.scalar.activation(to, ps_x[k % 2][:, :], ACT.Identity,
                                                        scale=mod_cur[:, u, 0, k:k + 1], bias=mod_cur[:, u, 1, k:k + 1])
                    last.then_inc(pipe.y_hi_ready, 1)

            end = runs_of(act)
            act.wait_ge(b1_in, 4 * DMA)
            act.wait_ge(table_out_out, DMA)
            cut_input(a, 0, None)
            for c in range(2):
                cut_w2(raw_w2, raw_w2_in, c)
            with act.Fori(0, end) as i:
                cut_hidden(a, i, b1_a, ACT.Gelu)
                cut_input(a, i + 1, None)

            last_tokens = tokens_of_last(act)
            with act.If(last_tokens <= P):
                cut_hidden(a, end, b1_a, ACT.Gelu, P)
            with act.Else():
                cut_hidden(a, end, b1_a, ACT.Gelu)
            act.wait_ge(ff_w1_in, DMA)
            act.wait_ge(b_mod_cur, 1)
            cut_input(b, 0, 0, lambda k: cut_w1(stage_raw, k))
            act.wait_ge(a.o_summed, end + 1)
            for c in range(2):
                cut_w2(raw_ff_w2, ff_w2_in, c)

            def step_b(s, u):
                cut_hidden(b, s, b1_b, ACT.Gelu_apprx_tanh)
                act.wait_ge(b_mod_cur, s + 2)
                cut_input(b, s + 1, 1 - u)

            with act.Fori(0, B // 2 - 1) as i:
                for u in range(2):
                    step_b(2 * i + u, u)
            step_b(B - 2, 0)
            cut_hidden(b, B - 1, b1_b, ACT.Gelu_apprx_tanh)

        @block.vector
        def _(dve):
            steps = [0]

            def link(ins):
                steps[0] += 1
                ins.then_inc(dve_step, 1)
                dve.wait_ge(dve_step, steps[0])

            dve.sem_inc(gated, FREE)

            nc.vector.memset(ones[:, :], 1.0)
            dve.wait_ge(mask_in, DMA)
            nc.vector.tensor_copy(mask_bf[:, :], mask_u8[:, :]).then_inc(mask_ready, 1)
            dve.wait_ge(consts_set, 5)
            nc.vector.tensor_scalar(upto[:, :], diff, 0.0, None, ALU.is_ge).then_inc(mask_ready, 1)
            nc.vector.tensor_scalar(before, diff, 0.0, None, ALU.is_gt).then_inc(mask_ready, 1)
            dve.wait_ge(totals_ps, 1)
            link(nc.vector.tensor_copy(total[:, :], ps_x[1][:, 0:1]))
            nc.vector.tensor_scalar(totals[:, :], ones[:, :], total[:, 0:1], None, ALU.mult).then_inc(totals_ready, 1)
            nc.vector.tensor_scalar(totals_before, before, total[:, 0:1], None,
                                    ALU.mult).then_inc(totals_ready, 1)
            bits_j, bits_s = J.bit_length() - 1, S.bit_length() - 1
            link(nc.vector.tensor_copy(col_bits[:, 0:1], col_no[:, :]))
            nc.vector.tensor_scalar(col_bits[:, 1:2], col_bits[:, 0:1], bits_j, bits_s, ALU.logical_shift_right,
                                    ALU.logical_shift_left)
            link(nc.vector.tensor_scalar(col_bits[:, 2:3], col_bits[:, 0:1], J - 1, None, ALU.bitwise_and))
            link(nc.vector.tensor_tensor(col_bits[:, 0:1], col_bits[:, 1:2], col_bits[:, 2:3], ALU.bitwise_or))
            dve.wait_ge(cond_turned, 1)
            nc.vector.tensor_copy(siluT, ps_o[3][:, 0:K * B].rearrange("p (k b) -> p k b", k=K)
                                  ).then_inc(siluT_ready, 1)
            dve.wait_ge(ranks_ps, 1)
            nc.vector.tensor_copy(finder[:, 0:P - 1], ps_h[0][:, 0:P - 1])
            link(nc.vector.tensor_copy(edges[:, 1:2], ps_h[0][:, P - 1:P]))
            link(nc.vector.tensor_tensor(edges[:, 0:1], edges[:, 1:2], total[:, :], ALU.subtract))
            link(nc.vector.tensor_copy(finder[:, P - 1:P], col_bits[:, 0:1]))

            def own(ins, steps, count):
                ins.then_inc(steps, 1)
                wait_alone(dve, steps, count)

            def choose_columns(t, column_of, scratch):
                own(nc.vector.tensor_scalar(scratch, slot_no[:, :], edges[:, 1:2], None, ALU.is_lt),
                    slot_cols, 3 * t + 1)
                own(nc.vector.scalar_tensor_tensor(out=column_of, in0=slot_no[:, :], scalar=edges[:, 0:1],
                                                   in1=scratch, op0=ALU.is_ge, op1=ALU.mult), slot_cols, 3 * t + 2)
                own(nc.vector.tensor_scalar(edges[:, :], edges[:, :], -float(S), None, ALU.add),
                    slot_cols, 3 * t + 3)

            def find_tokens(t, ps, scratch):
                found = ps.rearrange("p (j i) -> p j i", j=J)
                upto_slot = scratch.rearrange("p (j i) -> p j i", j=J)[:, :, 0:P - 1]
                wait_alone(dve, places_ps, t + 1)
                slot_of = slots[:, :].rearrange("p (j o) -> p j o", o=1).to_broadcast([P, J, P - 1])
                own(nc.vector.tensor_tensor(upto_slot, found[:, :, 0:P - 1], slot_of, ALU.is_le),
                    places_read, 4 * t + 1)
                own(nc.vector.tensor_reduce(place[:, :], upto_slot, AX.X, ALU.add), places_read, 4 * t + 2)
                tok = tok_no[:, bass.ds(J * t, J)]
                own(nc.vector.scalar_tensor_tensor(out=tok, in0=place[:, :], scalar=float(J),
                                                   in1=found[:, :, P - 1], op0=ALU.mult, op1=ALU.add),
                    places_read, 4 * t + 3)
                nc.vector.tensor_scalar(slots[:, :], slots[:, :], float(S), None, ALU.add)
                own(nc.vector.tensor_scalar(row_no[:, bass.ds(J * t, J)], tok, bits_s, None,
                                            ALU.logical_shift_right), places_read, 4 * t + 4)

            def copy_numbers(to, t):
                nc.vector.tensor_copy(to[:, 0, :], tok_no[:, bass.ds(J * t, J)])
                return nc.vector.tensor_copy(to[:, 1, :], row_no[:, bass.ds(J * t, J)])

            choose_columns(0, xhat[:, 0, :], xhat[:, 1, :])
            choose_columns(1, xhat[:, 2, :], xhat[:, 3, :])
            find_tokens(0, ps_x[0][:, :], xhat[:, 1, :])
            copy_numbers(idx_ln, 0).then_inc(a_idx_ln, 1)

            link(nc.vector.tensor_copy(runs_f[0:1, 0:1], ps_h[0][0:1, P:P + 1]))
            link(nc.vector.tensor_scalar(last_slot[0:1, 0:1], runs_f[0:1, 0:1], float(2 * S + 1), -1.0,
                                         ALU.max, ALU.add))
            link(nc.vector.tensor_scalar(last_slot[0:1, 1:2], last_slot[0:1, 0:1], bits_s, None,
                                         ALU.logical_shift_right))
            link(nc.vector.tensor_copy(runs[0:1, 0:1], last_slot[0:1, 1:2]))
            link(nc.vector.tensor_copy(runs_f[0:1, 3:4], runs[0:1, 0:1]))
            link(nc.vector.tensor_scalar(runs_f[0:1, 4:5], runs_f[0:1, 3:4], float(FEW - 1), float(C // J - FEW),
                                         ALU.is_gt, ALU.mult))
            link(nc.vector.tensor_scalar(runs[0:1, 1:2], runs_f[0:1, 4:5], float(FEW + 1), None, ALU.add))
            link(nc.vector.tensor_scalar(runs_f[0:1, 5:6], runs_f[0:1, 3:4], -float(S), None, ALU.mult))
            link(nc.vector.tensor_tensor(runs_f[0:1, 5:6], runs_f[0:1, 5:6], runs_f[0:1, 0:1], ALU.add))
            link(nc.vector.tensor_scalar(runs[0:1, 3:4], runs_f[0:1, 5:6], 1.0, None, ALU.max))
            link(nc.vector.tensor_scalar(runs_f[0:1, 3:4], runs_f[0:1, 3:4], 1.0, None, ALU.add))
            nc.vector.tensor_tensor(runs[0:1, 2:3], runs[0:1, 1:2], runs_f[0:1, 3:4],
                                    ALU.subtract).then_inc(runs_ready, 1)

            link(nc.vector.tensor_scalar(is_none, mask_bf[:, :], -(NONE + 1.0), NONE, ALU.mult, ALU.add))
            link(nc.vector.tensor_tensor(over_no[:, 0:C], ps_h[1][:, 0:C], is_none, ALU.add))

            def statistics(pipe, t, tokens):
                for j in range(J):
                    nc.vector.bn_stats(stats[:, j, :], tokens[:, j, :]).then_inc(pipe.stats_done, 1)
                wait_alone(dve, pipe.stats_done, J * t + J)
                for j in range(J):
                    nc.vector.bn_aggr(mean_var[:, j, :], stats[:, j, :]).then_inc(pipe.mean_done, 1)
                dve.wait_ge(pipe.mean_done, J * t + J)
                nc.vector.tensor_scalar(var_eps[:, :], mean_var[:, :, 1], EPS, None, ALU.add
                                        ).then_inc(pipe.var_ready, 1)

            def normal(j, tokens):
                return nc.vector.tensor_scalar(xhat[:, j, :], tokens[:, j, :], mean_var[:, j, 0:1], rstd[:, j:j + 1],
                                               ALU.subtract, ALU.mult)

            def low_input(pipe, t, first=lambda k: None):
                for k in range(K):
                    first(k)
                    dve.wait_ge(pipe.y_hi_ready, K * t + k + 1)
                    nc.vector.tensor_tensor(y_lo[:, k, :], full[:, 2 + k % 2, :], y_hi[:, k, :].bitcast(F32),
                                            ALU.subtract).then_inc(pipe.y_lo_ready, 1)

            def low_hidden(pipe, s, between, width=S):
                for m in range(M):
                    dve.wait_ge(pipe.h_hi_ready, M * s + m + 1)
                    nc.vector.tensor_tensor(h_lo[:, m, 0:width], full[:, m % 2, 0:width],
                                            h_hi[:, m, 0:width].bitcast(F32), ALU.subtract).then_inc(pipe.h_lo_ready, 1)
                    between(m)

            def low_w1(raw, chunks, k):
                dve.wait_ge(w1_hi_ready, chunks + k + 1)
                nc.vector.tensor_tensor(w1_lo[:, k, :], raw[:, k * HID:(k + 1) * HID],
                                        w1_hi[:, k, :].bitcast(F32), ALU.subtract).then_inc(w1_lo_ready, 1)

            def modulate_a(t):
                for j in range(J):
                    dve.wait_ge(a_tab_in[j], DMA * t + DMA)
                    dve.wait_ge(a_scaled, 2 * J * t + j + 1)
                    nc.vector.tensor_tensor(xhat[:, j, :], xhat[:, j, :], tab_ln[:, j, 0:D],
                                            ALU.mult).then_inc(a_scaled, 1)
                for j in range(J):
                    dve.wait_ge(a_scaled, 2 * J * t + J + j + 1)
                    nc.vector.tensor_tensor(xhat[:, j, :], xhat[:, j, :], tab_ln[:, j, D:2 * D],
                                            ALU.add).then_inc(a.xhat_ready, 1)

            def statistics_a(t):
                dve.wait_ge(a_x_in, J * DMA * t + J * DMA)
                statistics(a, t, xg)

            def normal_a(t):
                dve.wait_ge(a.rstd_ready, t + 1)
                for j in range(J):
                    normal(j, xg).then_inc(a_scaled, 1)

            dve.wait_ge(bias_in, 7 * DMA)
            link(nc.vector.tensor_tensor(rows_out[:, 1, :], rows_out[:, 1, :], b2_bwd, ALU.add))
            dve.wait_ge(ada_done, 1)
            link(nc.vector.tensor_tensor(rows_ln[:, 1, :], ps_o[0][0:B, :], rows_ln[:, 1, :], ALU.add))
            link(nc.vector.tensor_scalar(rows_ln[:, 0, :], rows_ln[:, 0, :], 1.0, None, ALU.add))
            dve.wait_ge(ada_done, 2)
            nc.vector.tensor_tensor(rows_ln[:, 0, :], ps_o[1][0:B, :], rows_ln[:, 0, :], ALU.add
                                    ).then_inc(rows_a_ready, 1)
            find_tokens(1, ps_x[1][:, :], xhat[:, 3, :])
            dve.wait_ge(ada_done, 3)
            link(nc.vector.tensor_tensor(rows_out[:, 0, :], ps_o[2][0:B, :], rows_out[:, 0, :], ALU.add))
            nc.vector.tensor_tensor(rows_out[:, 1, :], rows_out[:, 0, :], rows_out[:, 1, :], ALU.mult
                                    ).then_inc(rows_a_ready, 1)

            statistics_a(0)
            normal_a(0)
            for k in range(K):
                low_w1(raw_w1.rearrange("p t d -> p (t d)"), 0, k)

            for c in range(2):
                dve.wait_ge(ada_done, 4 + c)
                nc.vector.tensor_copy(shift_scale_b[:, c, :], ps_o[c][0:B, :]).then_inc(rows_b_ready, 1)

            modulate_a(0)
            copy_numbers(idx_ln, 1).then_inc(a_idx_ln, 1)

            dve.wait_ge(b1_in, 4 * DMA)
            link(nc.vector.tensor_scalar(mod_bias[:, 1, :], mod_bias[:, 1, :], 1.0, None, ALU.add))
            dve.wait_ge(mod_turned, 1)
            for c, to in enumerate((1, 0)):
                last = nc.vector.tensor_tensor(
                    mod_b[:, :, to, :],
                    ps_o[3][:, c * K * B:(c + 1) * K * B].rearrange("p (k b) -> p b k", k=K),
                    mod_bias[:, c:c + 1, :].to_broadcast([P, B, K]), ALU.add)
            last.then_inc(mod_ready, 1)
            dve.wait_ge(ada_done, 6)
            link(nc.vector.tensor_tensor(rows_b[:, 0, :], ps_o[2][0:B, :], rows_b[:, 0, :], ALU.add))
            nc.vector.tensor_tensor(rows_b[:, 1, :], rows_b[:, 0, :], rows_b[:, 1, :], ALU.mult
                                    ).then_inc(rows_b_ready, 1)
            low_input(a, 0)
            wait_alone(dve, a.y_lo_ready, K)
            choose_columns(2, full[:, 2, :], full[:, 3, :])

            def new_rows(i):
                dve.wait_ge(a_res_in, 2 * J * DMA * i + 2 * J * DMA)
                for j in range(J):
                    nc.vector.tensor_tensor(xr[:, j, :], xr[:, j, :], tab_out[:, j, D:2 * D],
                                            ALU.add).then_inc(a_biased, 1)
                dve.wait_ge(a.o_summed, i + 1)
                for j in range(J):
                    nc.vector.tensor_tensor(tab_out[:, j, 0:D], ps_o[j][:, :], tab_out[:, j, 0:D],
                                            ALU.mult).then_inc(gated, 1)
                for j in range(J):
                    dve.wait_ge(gated, J * i + j + 1 + FREE)
                    dve.wait_ge(a_biased, J * i + j + 1)
                    nc.vector.tensor_tensor(xr[:, j, :], xr[:, j, :], tab_out[:, j, 0:D],
                                            ALU.add).then_inc(a.out_ready, 1)

            def copy_current(t, u):
                nc.vector.tensor_copy(idx_over[:, :], over_no[:, bass.ds(J * t, J)]).then_inc(b_idx_over, 1)
                nc.vector.tensor_copy(mod_cur[:, u, :, :], mod_b[:, bass.ds(t, 1), :, :].rearrange(
                    "p o t k -> p (o t) k")).then_inc(b_mod_cur, 1)

            copy_current(0, 0)
            end = runs_of(dve)
            with dve.Fori(0, end) as i:
                copy_numbers(idx_out, i).then_inc(a_idx_out, 1)

                def between(m):
                    if m == 1:
                        find_tokens(i + 2, ps_x[0][:, :], full[:, 3, :])
                    if m == 2:
                        statistics_a(i + 1)
                    if m == 4:
                        normal_a(i + 1)

                low_hidden(a, i, between)
                modulate_a(i + 1)
                copy_numbers(idx_ln, i + 2).then_inc(a_idx_ln, 1)
                low_input(a, i + 1)
                wait_alone(dve, a.y_lo_ready, K * i + 2 * K)
                choose_columns(i + 3, full[:, 2, :], full[:, 3, :])
                new_rows(i)

            def statistics_b(t, u, in_count):
                dve.wait_ge(b_over_in, J * DMA * t + J * DMA)
                dve.wait_ge(b_gate_in[u], in_count)
                statistics(b, t, x_sb[u])

            def normal_b(t, u):
                dve.wait_ge(b.rstd_ready, t + 1)
                for j in range(J):
                    normal(j, x_sb[u]).then_inc(b.xhat_ready, 1)

            def add_bias(u):
                for j in range(J):
                    nc.vector.tensor_tensor(x_sb[u][:, j, :], x_sb[u][:, j, :], gate_sb[u][:, 1, :],
                                            ALU.add).then_inc(b_based, 1)

            copy_numbers(idx_out, end).then_inc(a_idx_out, 1)

            def between(m):
                if m == 1:
                    statistics_b(0, 0, DMA)
                if m == 2:
                    normal_b(0, 0)

            last_tokens = tokens_of_last(dve)
            with dve.If(last_tokens <= P):
                low_hidden(a, end, between, P)
            with dve.Else():
                low_hidden(a, end, between)
            low_input(b, 0, lambda k: low_w1(stage_raw, K, k))
            new_rows(end)
            add_bias(0)

            def gate_sub(u, j):
                nc.vector.tensor_tensor(o_sb[u][:, j, :], ps_o[j][:, :], gate_sb[u][:, 0, :], ALU.mult
                                        ).then_inc(gated, 1)

            def add_sub(s, u, j):
                dve.wait_ge(gated, J * s + J * end + J + j + 1 + FREE)
                nc.vector.tensor_tensor(o_sb[u][:, j, :], o_sb[u][:, j, :], x_sb[u][:, j, :],
                                        ALU.add).then_inc(b.out_ready, 1)

            def step_b(s, u, pair):
                copy_current(s + 1, 1 - u)

                def between(m):
                    if m == 3:
                        statistics_b(s + 1, 1 - u, DMA * (pair + 1) + DMA * u)
                    if m == 5:
                        normal_b(s + 1, 1 - u)

                low_hidden(b, s, between)
                add_bias(1 - u)
                low_input(b, s + 1)
                dve.wait_ge(b_stored[u], DMA * pair + FREE)
                dve.wait_ge(b.o_summed, s + 1)
                for j in range(J):
                    gate_sub(u, j)
                for j in range(J):
                    add_sub(s, u, j)

            with dve.Fori(0, B // 2 - 1) as i:
                for u in range(2):
                    step_b(2 * i + u, u, i)
            step_b(B - 2, 0, B // 2 - 1)
            low_hidden(b, B - 1, lambda m: None)
            dve.wait_ge(b_stored[1], DMA * (B // 2 - 1) + FREE)
            for j in range(J):
                dve.wait_ge(b.o_summed, B + j)
                gate_sub(1, j)
                add_sub(B - 1, 1, j)

        @block.tensor
        def _(pe):
            def warm(count, to):
                for _ in range(count):
                    nc.tensor.matmul(to[:, :], slot_no[:, 0:P], slot_no[:, :], start=True, stop=True)

            pe.wait_ge(consts_set, 5)
            warm(1, ps_o[2])
            pe.wait_ge(mask_ready, 3)
            nc.tensor.matmul(ps_x[1][:, 0:1], mask_bf[:, :], ones[:, 0:1], start=True, stop=True).then_inc(totals_ps, 1)
            pe.wait_ge(ident_ready, 1)
            pe.wait_ge(silu_done, 1)
            for k in range(K):
                last = nc.tensor.transpose(ps_o[3][:, B * k:B * k + B], silu_sb[:, P * k:P * k + P], ident[0:B, 0:B])
            last.then_inc(cond_turned, 1)
            pe.wait_ge(totals_ready, 2)
            nc.tensor.matmul(ps_h[0][:, 0:P], mask_bf[:, :], upto[:, :], start=True, stop=False)
            nc.tensor.matmul(ps_h[0][:, 0:P], before, totals[:, :], start=False, stop=True)
            nc.tensor.matmul(ps_h[0][0:1, P:P + 1], totals[:, 0:1], ones[:, 0:1], start=True, stop=True)
            nc.tensor.matmul(ps_h[1][:, 0:C], upto[:, :], mask_bf[:, :], start=True, stop=False)
            nc.tensor.matmul(ps_h[1][:, 0:C], ones[:, :], totals_before, start=False, stop=True
                             ).then_inc(ranks_ps, 1)

            def look_up(t, ps, column_of):
                pe.wait_ge(slot_cols, 3 * t + 2)
                for j in range(J):
                    last = nc.tensor.matmul(ps[:, P * j:P * j + P], column_of[:, P * j:P * j + P], finder[:, :],
                                            start=True, stop=True)
                last.then_inc(places_ps, 1)

            warm(1, ps_o[2])
            look_up(0, ps_x[0], xhat[:, 0, :])
            def modulation(first):
                for c in range(3):
                    pe.wait_ge(ada_in[first + c], DMA)
                    if first:
                        pe.wait_ge(rows_a_ready, 1 + c // 2)
                    for k in range(K):
                        last = nc.tensor.matmul(ps_o[c][0:B, :], siluT[:, k, :], stage[:, c, k, :],
                                                start=(k == 0), stop=(k == K - 1))
                    last.then_inc(ada_done, 1)
                    if not first and c == 0:
                        look_up(1, ps_x[1], xhat[:, 2, :])

            pe.wait_ge(siluT_ready, 1)
            modulation(0)
            end = runs_of(pe)
            last_tokens = tokens_of_last(pe)
            modulation(3)

            def turn_chunk(pipe, t, k):
                if k == 0:
                    pe.wait_ge(pipe.xhat_ready, J * t + J)
                if k >= 2:
                    pe.wait_ge(pipe.y_hi_ready, K * t + k - 1)
                for j in range(J):
                    last = nc.tensor.transpose(ps_x[k % 2][:, P * j:P * j + P], xhat[:, j, P * k:P * k + P], ident)
                last.then_inc(pipe.x_turned, 1)

            def layer1(pipe, s, chunks, width, between):
                for m in range(M):
                    if m >= 2:
                        pe.wait_ge(pipe.h_hi_ready, M * s + m - 1)
                    for k in range(K):
                        if m == 0:
                            pe.wait_ge(pipe.y_hi_ready, K * s + k + 1)
                            pe.wait_ge(pipe.y_lo_ready, K * s + k + 1)
                            pe.wait_ge(w1_hi_ready, chunks + k + 1)
                            pe.wait_ge(w1_lo_ready, chunks + k + 1)
                        w_hi, w_lo = w1_hi[:, k, P * m:P * m + P], w1_lo[:, k, P * m:P * m + P]
                        to, hi, lo = ps_h[m % 2][:, 0:width], y_hi[:, k, 0:width], y_lo[:, k, 0:width]
                        nc.tensor.matmul(to, w_hi, hi, start=(k == 0), stop=False)
                        nc.tensor.matmul(to, w_hi, lo, start=False, stop=False)
                        last = nc.tensor.matmul(to, w_lo, hi, start=False, stop=(k == K - 1))
                    last.then_inc(pipe.h_summed, 1)
                    between(m)

            def add_products(j, m):
                hi, lo = h_hi[:, m, P * j:P * j + P], h_lo[:, m, P * j:P * j + P]
                nc.tensor.matmul(ps_o[j][:, :], hi, w2_hi[:, m, :], start=(m == 0), stop=False)
                nc.tensor.matmul(ps_o[j][:, :], hi, w2_lo[:, m, :], start=False, stop=False)
                return nc.tensor.matmul(ps_o[j][:, :], lo, w2_hi[:, m, :], start=False, stop=(m == M - 1))

            def layer2(pipe, s, free, halves, subs, turn):
                pe.wait_ge(gated, free)
                for m in range(M):
                    if m % K == 0:
                        pe.wait_ge(w2_hi_ready, halves + m // K + 1)
                        pe.wait_ge(w2_lo_ready, halves + m // K + 1)
                    pe.wait_ge(pipe.h_hi_ready, M * s + m + 1)
                    pe.wait_ge(pipe.h_lo_ready, M * s + m + 1)
                    for j in range(subs):
                        last = add_products(j, m)
                    if m == M - 1:
                        last.then_inc(pipe.o_summed, 1)
                    if m in TURN_AFTER:
                        turn(TURN_AFTER.index(m))

            for c in range(2):
                pe.wait_ge(rows_b_ready, c + 1)
                for k in range(K):
                    last = nc.tensor.transpose(ps_o[3][:, (c * K + k) * B:(c * K + k + 1) * B],
                                               shift_scale_b[:, c, P * k:P * k + P], ident[0:B, 0:B])
            last.then_inc(mod_turned, 1)
            for k in range(K):
                turn_chunk(a, 0, k)
            pe.wait_ge(mod_ready, 1)
            pe.wait_ge(rows_b_ready, 3)
            with pe.Fori(0, end) as i:

                def between(m):
                    if m == 0:
                        look_up(i + 2, ps_x[0], full[:, 2, :])

                def turn(k):
                    if k == 0:
                        pe.wait_ge(places_read, 4 * i + 12)
                    turn_chunk(a, i + 1, k)

                layer1(a, i, 0, S, between)
                layer2(a, i, J * i + FREE, 0, J, turn)

            def last_supertile(width, subs):
                layer1(a, end, 0, width, lambda m: None)
                layer2(a, end, J * end + FREE, 0, subs, lambda k: turn_chunk(b, 0, k))

            with pe.If(last_tokens <= P):
                last_supertile(2 * P, 1)
            with pe.Else():
                last_supertile(S, J)

            def step_b(s):
                layer1(b, s, K, S, lambda m: None)
                layer2(b, s, J * s + J * end + J + FREE, 2, J, lambda k: turn_chunk(b, s + 1, k))

            with pe.Fori(0, B // 2 - 1) as i:
                for u in range(2):
                    step_b(2 * i + u)
            step_b(B - 2)
            layer1(b, B - 1, K, S, lambda m: None)
            wait_alone(pe, gated, J * (B - 1) + J * end + J + FREE)
            for j in range(J):
                for m in range(M):
                    if j == 0:
                        pe.wait_ge(b.h_hi_ready, M * (B - 1) + m + 1)
                        pe.wait_ge(b.h_lo_ready, M * (B - 1) + m + 1)
                    last = add_products(j, m)
                last.then_inc(b.o_summed, 1)


_INS = ['x', 'cond_1024', 'mask_BxS_bk0', 'L0_cond_ada_w', 'L0_cond_ada_b', 'L0_cond_ssm_w1', 'L0_cond_ssm_b1',
        'L0_cond_ssm_w2', 'L0_cond_ssm_b2', 'L0_cond_bwd_w1', 'L0_cond_bwd_b1', 'L0_cond_bwd_w2', 'L0_cond_bwd_b2',
        'L0_cond_ffada_w', 'L0_cond_ffada_b', 'L0_cond_ff_w1', 'L0_cond_ff_b1', 'L0_cond_ff_w2', 'L0_cond_ff_b2']


def kernel(**inputs):
    import numpy as _np
    import concourse.bacc as _bacc
    from concourse import mybir as _mybir
    from concourse.bass_utils import run_bass_kernel_spmd as _run

    nc = _bacc.Bacc("TRN2", target_bir_lowering=False, num_devices=1)
    arrays, args = {}, []
    for name in _INS:
        a = _np.ascontiguousarray(inputs[name])
        arrays[f"in_{name}"] = a
        args.append(nc.dram_tensor(f"in_{name}", a.shape, _mybir.dt.from_np(a.dtype), kind="ExternalInput").ap())
    shape = inputs['x'].shape
    args.append(nc.dram_tensor("out_0", shape, _mybir.dt.float32, kind="ExternalOutput").ap())
    build(nc, *args)
    r = _run(nc, [arrays], core_ids=[0])
    return r.results[0]["out_0"]
```
